# Optimizing a Trainium2 kernel written in Bass

```python
import numpy as np
import jax
import jax.numpy as jnp

def _softmax(x, axis=-1):
    return jax.nn.softmax(x, axis=axis)

def _gelu(x):
    return jax.nn.gelu(x, approximate=True)

def _silu(x):
    return jax.nn.silu(x)

def _sigmoid(x):
    return jax.nn.sigmoid(x)

def _layernorm(x, axis=-1, eps=1e-05):
    m = jnp.mean(x, axis=axis, keepdims=True)
    v = jnp.var(x, axis=axis, keepdims=True)
    return (x - m) / jnp.sqrt(v + eps)

def _scatter_add(tgt, idx, src, axis=0):
    return tgt.at[idx].add(src)

def _segment_sum(src, seg, n):
    return jax.ops.segment_sum(src, seg, n)
kernel_name = 'mk_prb_d2_jaxref_r8_7000af'

def setup_inputs(seed: int=0):
    np.random.seed(seed)
    _w = jnp.asarray

    def _L0_attn_setup():
        import jax, jax.numpy as jnp
        import numpy as np
        from jax import lax
        B, L, D, N, DT_RANK = (2, 256, 128, 16, 64)

        def _assoc_op(left, right):
            a_l, b_l = left
            a_r, b_r = right
            return (a_r * a_l, a_r * b_l + b_r)
        key = jax.random.key(seed)
        ks = jax.random.split(key, 6)
        x = jax.random.normal(ks[0], (B, L, D), dtype=jnp.float32)
        A_log = jnp.log(jnp.broadcast_to(jnp.arange(1, N + 1, dtype=jnp.float32), (D, N)))
        D_param = jnp.ones((D,), dtype=jnp.float32)
        W_bc = jax.random.normal(ks[1], (D, 2 * N), dtype=jnp.float32) / np.sqrt(D)
        W_dt = jax.random.normal(ks[2], (D, DT_RANK), dtype=jnp.float32) / np.sqrt(D)
        W_dtproj = jax.random.normal(ks[3], (DT_RANK, D), dtype=jnp.float32) / np.sqrt(DT_RANK)
        dt = jax.random.uniform(ks[4], (D,), minval=0.001, maxval=0.1, dtype=jnp.float32)
        b_dtproj = dt + jnp.log(-jnp.expm1(-dt))
        return {'x': x, 'A_log': A_log, 'D_param': D_param, 'W_bc': W_bc, 'W_dt': W_dt, 'W_dtproj': W_dtproj, 'b_dtproj': b_dtproj}
    _L0_attn_in = _L0_attn_setup()

    def _L0_ffn_setup():
        import jax, jax.numpy as jnp
        import numpy as np
        EMBED_DIM = 128
        HIDDEN_DIM = 512
        NUM_EXPERTS = 8
        TOP_K = 2
        key = jax.random.key(seed)
        k_x, k_g, k_w1, k_w2 = jax.random.split(key, 4)
        x = jax.random.normal(k_x, (2, 64, EMBED_DIM), dtype=jnp.float32)
        gate_w = jax.random.normal(k_g, (NUM_EXPERTS, EMBED_DIM), dtype=jnp.float32) * (1.0 / np.sqrt(EMBED_DIM))
        w1 = jax.random.normal(k_w1, (NUM_EXPERTS, EMBED_DIM, HIDDEN_DIM), dtype=jnp.float32) * np.sqrt(2.0 / EMBED_DIM)
        b1 = jnp.zeros((NUM_EXPERTS, HIDDEN_DIM), dtype=jnp.float32)
        w2 = jax.random.normal(k_w2, (NUM_EXPERTS, HIDDEN_DIM, EMBED_DIM), dtype=jnp.float32) * np.sqrt(2.0 / HIDDEN_DIM)
        b2 = jnp.zeros((NUM_EXPERTS, EMBED_DIM), dtype=jnp.float32)
        return {'x': x, 'gate_w': gate_w, 'w1': w1, 'b1': b1, 'w2': w2, 'b2': b2}
    _L0_ffn_in = _L0_ffn_setup()

    def _L1_attn_setup():
        import jax, jax.numpy as jnp
        import numpy as np
        DIMS = 128
        HEADS = 16
        HEAD_DIM = DIMS // HEADS
        key = jax.random.key(seed)
        k_x, k_q, k_k, k_v = jax.random.split(key, 4)
        scale = 1.0 / np.sqrt(DIMS)
        return {'input_seq_embs': jax.random.normal(k_x, (4, 512, DIMS), dtype=jnp.float32), 'W_Q': jax.random.normal(k_q, (DIMS, DIMS), dtype=jnp.float32) * scale, 'W_K': jax.random.normal(k_k, (DIMS, DIMS), dtype=jnp.float32) * scale, 'W_V': jax.random.normal(k_v, (DIMS, DIMS), dtype=jnp.float32) * scale}
    _L1_attn_in = _L1_attn_setup()

    def _L1_ffn_setup():
        import jax, jax.numpy as jnp
        import numpy as np
        D = 128
        E = 8
        K = 2
        DF = 512
        B, S = (2, 256)
        EPS_LN = 1e-05
        EPS_TOPK = 1e-08

        def _xavier(key, shape, fan_in, fan_out, dtype=jnp.float32):
            bound = float(np.sqrt(6.0 / (fan_in + fan_out)))
            return jax.random.uniform(key, shape, dtype, -bound, bound)
        key = jax.random.key(seed)
        kx, kg, k1, k2 = jax.random.split(key, 4)
        return {'x': jax.random.normal(kx, (B, S, D), jnp.float32), 'gamma': jnp.ones((D,), jnp.float32), 'beta': jnp.zeros((D,), jnp.float32), 'Wg': _xavier(kg, (E, D), D, E), 'bg': jnp.zeros((E,), jnp.float32), 'W1': _xavier(k1, (E, DF, D), D, DF), 'b1': jnp.zeros((E, DF), jnp.float32), 'W2': _xavier(k2, (E, D, DF), DF, D), 'b2': jnp.zeros((E, D), jnp.float32)}
    _L1_ffn_in = _L1_ffn_setup()
    _d = {'L0_attn_x': _L0_attn_in['x'], 'L0_attn_A_log': _L0_attn_in['A_log'], 'L0_attn_D_param': _L0_attn_in['D_param'], 'L0_attn_W_bc': _L0_attn_in['W_bc'], 'L0_attn_W_dt': _L0_attn_in['W_dt'], 'L0_attn_W_dtproj': _L0_attn_in['W_dtproj'], 'L0_attn_b_dtproj': _L0_attn_in['b_dtproj'], 'L0_ffn_gate_w': _L0_ffn_in['gate_w'], 'L0_ffn_w1': _L0_ffn_in['w1'], 'L0_ffn_b1': _L0_ffn_in['b1'], 'L0_ffn_w2': _L0_ffn_in['w2'], 'L0_ffn_b2': _L0_ffn_in['b2'], 'L1_attn_W_Q': _L1_attn_in['W_Q'], 'L1_attn_W_K': _L1_attn_in['W_K'], 'L1_attn_W_V': _L1_attn_in['W_V'], 'L1_ffn_gamma': _L1_ffn_in['gamma'], 'L1_ffn_beta': _L1_ffn_in['beta'], 'L1_ffn_Wg': _L1_ffn_in['Wg'], 'L1_ffn_bg': _L1_ffn_in['bg'], 'L1_ffn_W1': _L1_ffn_in['W1'], 'L1_ffn_b1': _L1_ffn_in['b1'], 'L1_ffn_W2': _L1_ffn_in['W2'], 'L1_ffn_b2': _L1_ffn_in['b2']}
    _x0 = _d['L0_attn_x']
    _d['L0_attn_x'] = jax.random.normal(jax.random.fold_in(jax.random.key(seed), 1), (16, 256, 128), dtype=_x0.dtype)
    del _x0
    return _d

def reference(L0_attn_x, L0_attn_A_log, L0_attn_D_param, L0_attn_W_bc, L0_attn_W_dt, L0_attn_W_dtproj, L0_attn_b_dtproj, L0_ffn_gate_w, L0_ffn_w1, L0_ffn_b1, L0_ffn_w2, L0_ffn_b2, L1_attn_W_Q, L1_attn_W_K, L1_attn_W_V, L1_ffn_gamma, L1_ffn_beta, L1_ffn_Wg, L1_ffn_bg, L1_ffn_W1, L1_ffn_b1, L1_ffn_W2, L1_ffn_b2):

    def _L0_attn_ref(x, A_log, D_param, W_bc, W_dt, W_dtproj, b_dtproj):
        import jax, jax.numpy as jnp
        import numpy as np
        from jax import lax
        B, L, D, N, DT_RANK = (2, 256, 128, 16, 64)

        def _assoc_op(left, right):
            a_l, b_l = left
            a_r, b_r = right
            return (a_r * a_l, a_r * b_l + b_r)
        x_bc = jnp.einsum('bld,dn->bln', x, W_bc)
        n = A_log.shape[1]
        B_sel = x_bc[..., :n]
        C_sel = x_bc[..., n:]
        dt_low = jnp.einsum('bld,dr->blr', x, W_dt)
        delta = jax.nn.softplus(jnp.einsum('blr,rd->bld', dt_low, W_dtproj) + b_dtproj)
        A = -jnp.exp(A_log)
        A_bar = jnp.exp(delta[..., None] * A)
        Bx = (delta * x)[..., None] * B_sel[:, :, None, :]
        _, all_h = lax.associative_scan(_assoc_op, (A_bar, Bx), axis=1)
        y = jnp.sum(C_sel[:, :, None, :] * all_h, axis=-1)
        return y + D_param * x

    def _L0_ffn_ref(x, gate_w, w1, b1, w2, b2):
        import jax, jax.numpy as jnp
        import numpy as np
        EMBED_DIM = 128
        HIDDEN_DIM = 512
        NUM_EXPERTS = 8
        TOP_K = 2
        orig_shape = x.shape
        xt = x.reshape(-1, EMBED_DIM)
        logits = xt @ gate_w.T
        probs = jax.nn.softmax(logits, axis=-1)
        top_w, top_i = jax.lax.top_k(probs, TOP_K)
        top_w = top_w / (top_w.sum(axis=-1, keepdims=True) + 1e-09)
        h = jnp.einsum('td,ndh->tnh', xt, w1) + b1
        h = jax.nn.gelu(h, approximate=False)
        out_all = jnp.einsum('tnh,nhd->tnd', h, w2) + b2
        sel = jnp.take_along_axis(out_all, top_i[:, :, None], axis=1)
        out = (sel * top_w[:, :, None]).sum(axis=1)
        return out.reshape(orig_shape)

    def _L1_attn_ref(input_seq_embs, W_Q, W_K, W_V):
        import jax, jax.numpy as jnp
        import numpy as np
        DIMS = 128
        HEADS = 16
        HEAD_DIM = DIMS // HEADS
        B, L, d = input_seq_embs.shape
        H, hd = (HEADS, HEAD_DIM)
        Q = (input_seq_embs @ W_Q.T).reshape(B, L, H, hd)
        K = (input_seq_embs @ W_K.T).reshape(B, L, H, hd)
        V = (input_seq_embs @ W_V.T).reshape(B, L, H, hd)
        sK = jax.nn.softmax(jnp.swapaxes(K, -1, -2), axis=-1)
        tran_V = jnp.einsum('bldh,blhe->blde', sK, V)
        out = jnp.einsum('blhd,blde->blhe', jax.nn.softmax(Q, axis=-1), tran_V)
        return out.reshape(B, L, d)

    def _L1_ffn_ref(x, gamma, beta, Wg, bg, W1, b1, W2, b2):
        import jax, jax.numpy as jnp
        import numpy as np
        D = 128
        E = 8
        K = 2
        DF = 512
        B, S = (2, 256)
        EPS_LN = 1e-05
        EPS_TOPK = 1e-08

        def _xavier(key, shape, fan_in, fan_out, dtype=jnp.float32):
            bound = float(np.sqrt(6.0 / (fan_in + fan_out)))
            return jax.random.uniform(key, shape, dtype, -bound, bound)
        b, s, d = x.shape
        mu = jnp.mean(x, axis=-1, keepdims=True)
        var = jnp.mean((x - mu) ** 2, axis=-1, keepdims=True)
        xn = (x - mu) / jnp.sqrt(var + EPS_LN) * gamma + beta
        xf = xn.reshape(-1, d)
        logits = xf @ Wg.T + bg
        probs = jax.nn.softmax(logits, axis=-1)
        tp, ti = jax.lax.top_k(probs, K)
        tp = tp / (jnp.sum(tp, axis=-1, keepdims=True) + EPS_TOPK)
        w = jnp.sum(jax.nn.one_hot(ti, E, dtype=xf.dtype) * tp[..., None], axis=1)
        h = jax.nn.gelu(jnp.einsum('td,efd->tef', xf, W1) + b1, approximate=False)
        y = jnp.einsum('tef,edf->ted', h, W2) + b2
        out = jnp.einsum('ted,te->td', y, w)
        return x + out.reshape(b, s, d)
    x = L0_attn_x
    xn = _layernorm(x, axis=-1)
    x = x + _L0_attn_ref(xn, L0_attn_A_log, L0_attn_D_param, L0_attn_W_bc, L0_attn_W_dt, L0_attn_W_dtproj, L0_attn_b_dtproj) + _L0_ffn_ref(xn, L0_ffn_gate_w, L0_ffn_w1, L0_ffn_b1, L0_ffn_w2, L0_ffn_b2)
    xn = _layernorm(x, axis=-1)
    x = x + _L1_attn_ref(xn, L1_attn_W_Q, L1_attn_W_K, L1_attn_W_V) + _L1_ffn_ref(xn, L1_ffn_gamma, L1_ffn_beta, L1_ffn_Wg, L1_ffn_bg, L1_ffn_W1, L1_ffn_b1, L1_ffn_W2, L1_ffn_b2)
    return x

_drawn_inputs = setup_inputs


def setup_inputs(seed=0):
    import zlib

    import numpy as np

    out = dict(_drawn_inputs(seed))
    spreads = {'L0_attn_D_param': (1.0, 0.2),
     'L0_ffn_b1': (0.0, 0.1),
     'L0_ffn_b2': (0.0, 0.1),
     'L1_ffn_gamma': (1.0, 0.2),
     'L1_ffn_beta': (0.0, 0.344),
     'L1_ffn_bg': (0.0, 0.346),
     'L1_ffn_b1': (0.0, 0.442),
     'L1_ffn_b2': (0.0, 0.355)}
    factors = {}
    for name, (base, spread) in spreads.items():
        noise = np.random.default_rng([zlib.crc32(name.encode()), seed]).standard_normal(out[name].shape)
        drawn = base * np.exp(spread * noise) if base else spread * noise
        out[name] = jnp.asarray(drawn.astype(out[name].dtype))
    for name, factor in factors.items():
        out[name] = (out[name] * factor).astype(out[name].dtype)
    return out
```

```python
from contextlib import ExitStack, contextmanager

import concourse.bass as bass
from concourse import mybir

ALU = mybir.AluOpType
ACT = mybir.ActivationFunctionType
AX_X = mybir.AxisListType.X
F32, F16, BF16 = mybir.dt.float32, mybir.dt.float16, mybir.dt.bfloat16
I32, U32 = mybir.dt.int32, mybir.dt.uint32

P = 128
SEQ, SLEN, D = 16, 256, 128
NTOK = SEQ * SLEN
TILES = NTOK // P
GROUPS = 8
TG = TILES // GROUPS
GC = TG * P
NS = 16
RANK = 64
NE = 8
HID = 512
HC = HID // P
HEADS, HD = 16, 8
LN_EPS = 1e-5
TOP_EPS = (1e-9, 1e-8)
BLOCKS = 72
FIRST = 2
BPG = BLOCKS // (GROUPS - FIRST)
ROWF = 2 * D + 2
XR = 6
assert BLOCKS >= 2 * TILES + NE - 1 and BPG % XR == 0


class Steps:

    def __init__(self, eng, sem):
        self.eng, self.sem, self.n, self.off = eng, sem, 0, 0

    def done(self, ins):
        ins.then_inc(self.sem, 1)
        self.n += 1

    def wait(self):
        self.eng.wait_ge(self.sem, self.off + self.n)

    def seq(self, ins):
        self.done(ins)
        self.wait()

    @contextmanager
    def loop(self, first, end, per):
        n0 = self.n
        with self.eng.Fori(first, end) as i:
            self.off = (i - first) * per
            yield i
        assert self.n == n0 + per, (self.n - n0, per)
        self.n, self.off = n0 + per * (end - first), 0


def hold_of(eng, held):
    return lambda: eng.sem_inc(held, 1)


def build(nc, a, out):
    ctx = ExitStack()
    with ctx:
        def sb(name, shape, dt=F32):
            return ctx.enter_context(nc.sbuf_tensor(name, shape, dt))

        def ps(name, shape, dt=F32):
            return ctx.enter_context(nc.psum_tensor(name, shape, dt))

        def sem(name):
            return ctx.enter_context(nc.semaphore(name))

        def dram(name, shape, dt):
            return nc.dram_tensor(name, shape, dt, kind="Internal").ap()

        slots_dram = [dram(f"slots{l}", [BLOCKS * P, ROWF], F16) for l in range(2)]
        NRES = 2 * NTOK
        res_dram = [dram(f"results{l}", [NRES, D], F32) for l in range(2)]

        x = sb("x", [P, TILES, D])
        xT = sb("xT", [P, NTOK])
        big = sb("big", [P, NTOK])
        parts = sb("parts", [P, NTOK], BF16)
        rows = sb("rows", [P, TILES, ROWF], F16)
        decay = sb("decay", [P, NS, GC])
        work = sb("work", [P, 8, GC])
        w1h = sb("w1h", [P, 2 * NE * HID], F16)
        w1l = sb("w1l", [P, 2 * NE * HID], F16)
        w2h = sb("w2h", [P, 2 * NE * HID], F16)
        w2l = sb("w2l", [P, 2 * NE * HID], F16)
        xrow = sb("xrow", [P, XR, ROWF], F16)
        xrT = sb("xrT", [P, 2, 2 * D], F16)
        hid = sb("hid", [P, 2, HID])
        hid_h = sb("hid_h", [P, 2, HID], F16)
        hid_l = sb("hid_l", [P, 2, HID], F16)
        res = sb("res", [P, XR, D])
        b1 = sb("b1", [P, 2 * NE * HC])
        idf = sb("idf", [P, P])
        idh = sb("idh", [P, P], F16)
        upper = sb("upper", [P, P], BF16)
        ones = sb("ones", [P, P], BF16)
        pick = sb("pick", [96, 2 * NS], BF16)
        wbc = sb("wbc", [P, 96])
        wdt = sb("wdt", [P, RANK])
        wdp = sb("wdp", [RANK, D])
        gate = sb("gate", [P, 2, NE])
        cols = sb("cols", [P, 2 + NS])
        avec = sb("avec", [P, NS])
        bgate = sb("bgate", [P, NE])
        stats = sb("stats", [P, TILES, 6])
        mean = sb("mean", [P, TILES])
        vare = sb("vare", [P, TILES])
        rstd = sb("rstd", [P, TILES])
        ntmp = sb("ntmp", [P, TILES])
        logits = sb("logits", [P, TILES, NE])
        mask = sb("mask", [P, TILES * NE], BF16)
        count_i = sb("count_i", [P, BLOCKS], I32)
        count = sb("count", [P, BLOCKS])
        topw = sb("topw", [P, 2, TILES])
        slot = sb("slot", [P, 2, TILES], I32)
        eid = sb("eid", [1, BLOCKS], I32)

        pb = ps("pb", [P, 4, GC])
        py = ps("py", [P, GC])
        px = ps("px", [P, 2 * D], F16)
        ph = ps("ph", [P, HID])
        po = ps("po", [P, GC])

        s_x = sem("s_x")
        s_small = sem("s_small")
        s_late = sem("s_late")
        s_b2 = sem("s_b2")
        s_stage = [sem(f"s_stage{i}") for i in range(8)]
        s_zeroed = [sem(f"s_zeroed{l}") for l in range(2)]
        s_disp = [sem(f"s_disp{l}") for l in range(2)]
        s_row = [sem(f"s_row{i}") for i in range(XR)]
        s_sent = [sem(f"s_sent{i}") for i in range(XR)]
        s_back = [sem(f"s_back{i}") for i in range(2)]
        s_out = sem("s_out")
        s_pool = sem("s_pool")
        s_act = sem("s_act")
        s_dve = sem("s_dve")
        s_const = sem("s_const")
        s_ones = sem("s_ones")
        s_held = [sem(f"s_held{i}") for i in range(3)]
        s_aexp = sem("s_aexp")
        s_avec = sem("s_avec")
        s_whi, s_wlo = sem("s_whi"), sem("s_wlo")
        s_var, s_rstd = sem("s_var"), sem("s_rstd")
        s_xn = sem("s_xn")
        s_xnT = sem("s_xnT")
        s_xT = sem("s_xT")
        s_lg, s_lgout = sem("s_lg"), sem("s_lgout")
        s_bc, s_parts = sem("s_bc"), sem("s_parts")
        s_low, s_lowout = sem("s_low"), sem("s_lowout")
        s_pre = sem("s_pre")
        s_soft = sem("s_soft")
        s_delta = sem("s_delta")
        s_rhi = sem("s_rhi")
        s_rlo = sem("s_rlo")
        s_mask, s_rank = sem("s_mask"), sem("s_rank")
        s_expin, s_expout = sem("s_expin"), sem("s_expout")
        s_topw = sem("s_topw")
        s_slot = sem("s_slot")
        s_bb, s_cb = sem("s_bb"), sem("s_cb")
        s_bx = sem("s_bx")
        s_a = sem("s_a")
        s_scan = sem("s_scan")
        s_prod = sem("s_prod")
        s_ysum = sem("s_ysum")
        s_yT, s_yTT = sem("s_yT"), sem("s_yTT")
        s_att = sem("s_att")
        s_xr, s_xrout = sem("s_xr"), sem("s_xrout")
        s_l1, s_gelu, s_hl = sem("s_l1"), sem("s_gelu"), sem("s_hl")
        s_l2, s_res = sem("s_l2"), sem("s_res")
        s_x1 = sem("s_x1")
        s_add = sem("s_add")
        s_xf, s_gb = sem("s_xf"), sem("s_gb")
        s_xg = sem("s_xg")
        s_qkv, s_v = sem("s_qkv"), sem("s_v")
        s_qks, s_qke = sem("s_qks"), sem("s_qke")
        s_p1, s_tsum = sem("s_p1"), sem("s_tsum")
        block = ctx.enter_context(nc.Block())

        decay_all = decay[:, :, :].rearrange("p a c -> p (a c)")
        stage = decay_all.rearrange("p (s c) -> p s c", s=8)
        rows_id = rows[:, :, :].rearrange("p t c -> p (t c)").bitcast(I32).rearrange(
            "p (t c) -> p t c", t=TILES)[:, :, D]
        b2 = rows[:, :, :].rearrange("p t c -> p (t c)").bitcast(F32)[:, 0:NE * D]
        parts_f = parts[:, :].bitcast(F32)
        wqkv = parts_f[:, 0:3 * D]
        gb = parts_f[:, 3 * D:5 * D].rearrange("p (k d) -> p k d", k=2)
        fill = xrow[:, 0, :]
        tmp_a = hid_h[:, :, :].rearrange("p r c -> p (r c)").bitcast(F32)
        tmp_b = hid_l[:, :, :].rearrange("p r c -> p (r c)").bitcast(F32)
        yT = work[:, 7, :]
        xTg = work[:, 6, :]
        fill_id = fill[:, :].bitcast(I32)[:, D:D + 1]
        work_all = work[:, :, :].rearrange("p a c -> p (a c)")
        xn = work_all.rearrange("p (t c) -> p t c", c=D)
        x_all = x[:, :, :].rearrange("p t c -> p (t c)")
        xf = big[:, :].rearrange("p (t c) -> p t c", t=TILES)
        logits_all = logits[:, :, :].rearrange("p t k -> p (t k)")
        low = res[:, :, :].rearrange("p r c -> p (r c)")[0:RANK, 0:GC]
        product = decay_all.rearrange("p (k t c) -> p k t c", k=2, t=TG)
        SMALL = 13

        def ids_of(r):
            return xrow[:, r, :].bitcast(I32)[:, D:D + 1]

        def group(g):
            return bass.ds(g * GC, GC)

        def tile(g, t):
            return bass.ds(g * GC + t * P, P)

        def col(i):
            return bass.ds(i, 1)

        def blockno(l, g, j):
            return (g - FIRST) * BPG + (j + l * BLOCKS)

        def turn(l, g, j):
            return (g - FIRST) * (BPG // XR) + (j // XR + l * (BLOCKS // XR))

        def expert(e, g, j):
            return e.value_load(eid[0:1, col((g - FIRST) * BPG + j)], min_val=0, max_val=NE - 1)

        @block.sync
        def _(e):
            e.dma_start(x[:, :, :], a["x"].rearrange("(t p) d -> p t d", p=P)).then_inc(s_x, 16)
            small = [(wbc[:, 32 * q:32 * q + 32], a["W_bc"]) for q in range(3)]
            small += [(wdt[:, :], a["W_dt"]), (wdp[:, :], a["W_dtproj"]), (gate[:, 0, :], a["gate_0"]),
                      (gate[:, 1, :], a["gate_1"]), (cols[:, 0:1], a["b_dt"]),
                      (cols[:, 1:2], a["D_param"]), (cols[:, 2:2 + NS], a["A_log"]),
                      (b1[:, 0:NE * HC], a["b1_0"]), (b1[:, NE * HC:2 * NE * HC], a["b1_1"]),
                      (bgate[:, :], a["bg"].to_broadcast([P, NE]))]
            assert len(small) == SMALL
            for dst, src in small:
                e.dma_start(dst, src).then_inc(s_small, 16)
            for i in range(2 * NE):
                l, n = i // NE, i % NE
                if i >= 8:
                    e.wait_ge(s_wlo, i - 7)
                e.dma_start(stage[:, i % 8, 0:HID], a[f"w1_{l}"][n]).then_inc(s_stage[i % 8], 16)
                e.dma_start(stage[:, i % 8, HID:2 * HID], a[f"w2_{l}"][n]).then_inc(s_stage[i % 8], 16)
            e.wait_ge(s_const, 1)
            for l in range(2):
                e.dma_start(slots_dram[l].rearrange("(b p) c -> p b c", p=P),
                            fill[:, :].unsqueeze(1).to_broadcast([P, BLOCKS, ROWF])).then_inc(s_zeroed[l], 16)

            for l in range(2):
                e.wait_ge(s_disp[l], 16 * 2 * TILES)
                e.dma_start(b2, a[f"b2_{l}"].to_broadcast([P, NE * D])).then_inc(s_b2, 16)

                def block_rows(g, j, used):
                    if used:
                        e.wait_ge(s_sent[j % XR], turn(l, g, j) * 16)
                    e.dma_start(xrow[:, j % XR, :], slots_dram[l][bass.ds(blockno(0, g, j) * P, P), :])\
                        .then_inc(s_row[j % XR], 16)

                for j in range(BPG):
                    block_rows(FIRST, j, l * BPG + j >= XR)
                with e.Fori(FIRST + 1, GROUPS) as g:
                    for j in range(BPG):
                        block_rows(g, j, True)
                for r in range(XR):
                    e.wait_ge(s_sent[r], 16 * (l + 1) * (BLOCKS // XR))
                e.wait_ge(s_att, (l + 1) * GROUPS + 1)
                if l == 0:
                    for dst, src in ((wqkv, a["wqkv"]), (gb[:, 0, :], a["gamma"].to_broadcast([P, D])),
                                     (gb[:, 1, :], a["beta"].to_broadcast([P, D]))):
                        e.dma_start(dst, src).then_inc(s_late, 16)
                with e.Fori(0, GROUPS // 2) as pair:
                    for par in range(2):
                        gg = pair * 2
                        e.wait_ge(s_x1, gg + (par + 1 + l * GROUPS))
                        for k in range(2):
                            e.dma_start(decay[:, 2 * par + k, :].rearrange("p (t c) -> p t c", t=TG),
                                        res_dram[l][bass.ds((gg + par) * GC + k * NTOK, GC), :].rearrange(
                                            "(t p) c -> p t c", p=P)).then_inc(s_back[par], 16)

        @block.gpsimd
        def _(e):
            st = Steps(e, s_pool)
            hold = hold_of(e, s_held[0])
            e.memset(ones[:, :], 1.0).then_inc(s_ones, 1)
            e.memset(idf[:, :], 0.0)
            e.memset(idh[:, :], 0.0)
            e.memset(upper[:, :], 1.0)
            e.memset(pick[:, :], 0.0)
            e.iota(count_i[:, :], pattern=[[1, BLOCKS]], base=0, channel_multiplier=0)
            st.seq(e.memset(fill[:, :], 0.0))
            e.affine_select(out=idf[:, :], in_=idf[:, :], compare_op=ALU.not_equal, fill=1.0, base=0,
                            pattern=[[-1, P]], channel_multiplier=1)
            e.affine_select(out=idh[:, :], in_=idh[:, :], compare_op=ALU.not_equal, fill=1.0, base=0,
                            pattern=[[-1, P]], channel_multiplier=1)
            e.affine_select(out=upper[:, :], in_=upper[:, :], compare_op=ALU.is_gt, fill=0.0, base=0,
                            pattern=[[1, P]], channel_multiplier=-1)
            e.iota(fill_id, pattern=[[0, 1]], base=NRES, channel_multiplier=0)
            for q in range(3):
                st.seq(e.affine_select(out=pick[:, :], in_=pick[:, :], compare_op=ALU.not_equal, fill=1.0,
                                       base=-32 * q, pattern=[[-1, 2 * NS]], channel_multiplier=1))
            e.memset(eid[:, :], 0).then_inc(s_const, 1)
            def rows_low(l, g):
                hi, lo = (rows[:, bass.ds(g * TG, TG), k * D:(k + 1) * D] for k in range(2))
                e.tensor_tensor(lo, (xf if l else xn)[:, bass.ds(g * TG, TG), :], hi, ALU.subtract).then_inc(s_rlo, 1)

            for i in range(2 * NE):
                if i % 2 == 0:
                    e.wait_ge(s_rhi, i // 2 + 1)
                    rows_low(0, i // 2)
                e.wait_ge(s_whi, i + 1)
                sl = slice(i * HID, (i + 1) * HID)
                e.tensor_tensor(w1l[:, sl], stage[:, i % 8, 0:HID], w1h[:, sl], ALU.subtract)
                e.tensor_tensor(w2l[:, sl], stage[:, i % 8, HID:2 * HID], w2h[:, sl], ALU.subtract).then_inc(s_wlo, 1)

            for l in range(2):
                if l == 1:
                    with e.Fori(0, GROUPS) as g:
                        e.wait_ge(s_xn, g + (GROUPS + 1))
                        hold()
                        e.tensor_tensor(x_all[:, group(g)], x_all[:, group(g)], work_all[:, group(g)],
                                        ALU.add).then_inc(s_add, 1)
                    e.wait_ge(s_late, 48)
                    with st.loop(0, GROUPS, 1) as g:
                        gt = xf[:, bass.ds(g * TG, TG), :]
                        e.wait_ge(s_xf, g + 1)
                        hold()
                        st.seq(e.tensor_tensor(gt, gt, gb[:, 0:1, :].to_broadcast([P, TG, D]), ALU.mult))
                        hold()
                        e.tensor_tensor(gt, gt, gb[:, 1:2, :].to_broadcast([P, TG, D]), ALU.add).then_inc(s_gb, 1)
                        e.wait_ge(s_rhi, g + (GROUPS + 1))
                        hold()
                        rows_low(1, g)
                st.seq(e.iota(rows_id, pattern=[[P, TILES]], base=0, channel_multiplier=1))
                e.wait_ge(s_rlo, (l + 1) * GROUPS)
                e.wait_ge(s_zeroed[l], 16)
                e.wait_ge(s_slot, l + 1)
                for k in range(2):
                    for t in range(TILES):
                        e.indirect_dma_start(slots_dram[l], bass.IndirectOffsetOnAxis(slot[:, k, t:t + 1], 0),
                                             rows[:, t, :], None).then_inc(s_disp[l], 16)
                    if k == 0:
                        e.wait_ge(s_disp[l], 16 * TILES)
                        st.seq(e.iota(rows_id, pattern=[[P, TILES]], base=NTOK, channel_multiplier=1))
                with e.Fori(FIRST, GROUPS) as g:
                    for j in range(BPG):
                        e.wait_ge(s_res, blockno(l, g, j) + 2)
                        hold()
                        e.indirect_dma_start(res_dram[l], bass.IndirectOffsetOnAxis(ids_of(j % XR), 0),
                                             res[:, j % XR, :], None, bounds_check=NRES - 1,
                                             oob_is_err=False).then_inc(s_sent[j % XR], 16)

        @block.scalar
        def _(e):
            st = Steps(e, s_act)
            hold = hold_of(e, s_held[1])
            for free in (s_xrout, s_gelu, s_v):
                e.sem_inc(free, 1)
            e.wait_ge(s_small, 16 * SMALL)
            e.activation(avec[:, :], cols[:, 2:2 + NS], ACT.Exp).then_inc(s_aexp, 1)

            def rstd_of(n):
                e.wait_ge(s_var, n)
                st.seq(e.activation(ntmp[:, :], vare[:, :], ACT.Ln))
                e.activation(rstd[:, :], ntmp[:, :], ACT.Exp, scale=-0.5).then_inc(s_rstd, 1)

            def gate_exp(n):
                e.wait_ge(s_expin, n)
                e.activation(logits_all, logits_all, ACT.Exp).then_inc(s_expout, 1)

            rstd_of(1)

            def channels_out(g):
                e.wait_ge(s_xnT, g + 1)
                e.copy(xT[:, group(g)], py[:, :]).then_inc(s_xT, 1)

            def rows_high(l, g):
                hi = rows[:, bass.ds(g * TG, TG), 0:D]
                if l == 0:
                    e.wait_ge(s_xn, g + 1)
                    e.copy(hi, xn[:, bass.ds(g * TG, TG), :]).then_inc(s_rhi, 1)
                else:
                    e.wait_ge(s_gb, g + 1)
                    hold()
                    e.copy(hi, xf[:, bass.ds(g * TG, TG), :]).then_inc(s_rhi, 1)

            def low_out(g):
                e.wait_ge(s_low, g + 1)
                if g > 0:
                    e.wait_ge(s_pre, g)
                e.copy(low, pb[0:RANK, 3, :]).then_inc(s_lowout, 1)

            def softplus(g):
                e.wait_ge(s_pre, g + 1)
                st.seq(e.activation(tmp_a[:, :], ph[:, :], ACT.Abs, bias=cols[:, 0:1]))
                st.seq(e.activation(tmp_a[:, :], tmp_a[:, :], ACT.Exp, scale=-1.0))
                e.wait_ge(s_delta, g + 1)
                e.activation(tmp_b[:, :], tmp_a[:, :], ACT.Ln, bias=1.0).then_inc(s_soft, 1)

            def weights_high(i):
                e.wait_ge(s_stage[i % 8], 32 * (i // 8 + 1))
                sl = slice(i * HID, (i + 1) * HID)
                e.copy(w1h[:, sl], stage[:, i % 8, 0:HID])
                e.copy(w2h[:, sl], stage[:, i % 8, HID:2 * HID]).then_inc(s_whi, 1)

            channels_out(0)
            for g in range(GROUPS):
                rows_high(0, g)
                low_out(g)
                weights_high(2 * g)
                if g + 1 < GROUPS:
                    channels_out(g + 1)
                softplus(g)
                weights_high(2 * g + 1)
            gate_exp(1)

            def decays(g):
                for n in range(NS):
                    e.wait_ge(s_scan, g * NS + (n + 1))
                    hold()
                    e.activation(decay[:, n, :], big[:, group(g)], ACT.Exp, scale=avec[:, n:n + 1]).then_inc(s_a, 1)

            def block_in(l, g, j):
                e.wait_ge(s_xr, blockno(l, g, j) + 1)
                e.copy(xrT[:, j % 2, :], px[:, :]).then_inc(s_xrout, 1)

            def block_gelu(l, g, j):
                en = expert(e, g, j)
                e.wait_ge(s_hl, blockno(l, g, j) + 1)
                e.wait_ge(s_l1, blockno(l, g, j) + 1)
                hold()
                for c in range(HC):
                    ins = e.activation(hid[:, j % 2, c * P:(c + 1) * P], ph[:, c * P:(c + 1) * P], ACT.Gelu,
                                       bias=b1[:, col(en * HC + (l * NE * HC + c))])
                ins.then_inc(s_gelu, 1)

            def blocks(l, g):
                block_in(l, g, 0)
                for j in range(BPG):
                    if j + 1 < BPG:
                        block_in(l, g, j + 1)
                    block_gelu(l, g, j)

            e.wait_ge(s_wlo, 2 * NE)
            e.wait_ge(s_avec, 1)
            decays(0)
            with e.Fori(0, FIRST) as g:
                decays(g + 1)
            with e.Fori(FIRST, GROUPS - 1) as g:
                blocks(0, g)
                decays(g + 1)
            blocks(0, GROUPS - 1)

            rstd_of(2)
            with e.Fori(0, GROUPS) as g:
                e.wait_ge(s_xnT, g + (GROUPS + 1))
                hold()
                e.copy(xT[:, group(g)], py[:, :]).then_inc(s_xT, 1)
            rstd_of(3)
            with e.Fori(0, GROUPS) as g:
                e.wait_ge(s_xnT, g + (2 * GROUPS + 1))
                e.wait_ge(s_lg, g + GROUPS)
                e.copy(tmp_a[:, :], py[:, :]).then_inc(s_xT, 1)
                rows_high(1, g)
            gate_exp(2)

            def head_input(g):
                e.wait_ge(s_qkv, g + 1)
                hold()
                e.copy(xTg, xT[:, group(g)]).then_inc(s_xg, 1)

            def head_exps(g):
                e.wait_ge(s_qkv, g + 2)
                e.copy(work[:, 2, :].rearrange("p (t c) -> p t c", t=TG), pb[:, :, 2 * D:3 * D]).then_inc(s_v, 1)
                for k in range(2):
                    e.wait_ge(s_qks, g * 2 + (k + 2))
                    e.activation(work[:, k, :], work[:, k, :], ACT.Exp).then_inc(s_qke, 1)

            e.wait_ge(s_topw, 2)
            with e.Fori(0, FIRST) as g:
                head_input(g)
                head_exps(g)
            with e.Fori(FIRST, GROUPS) as g:
                head_input(g)
                head_exps(g)
                blocks(1, g)
            with e.Fori(0, GROUPS) as g:
                e.wait_ge(s_x1, g + (GROUPS + 3))
                e.dma_start(out[bass.ds(g * GC, GC), :].rearrange("(t p) d -> p t d", p=P),
                            x[:, bass.ds(g * TG, TG), :]).then_inc(s_out, 16)
            e.wait_ge(s_out, 16 * GROUPS)

        @block.tensor
        def _(e):
            e.sem_inc(s_qkv, 1)
            e.wait_ge(s_const, 1)
            e.wait_ge(s_small, 16 * SMALL)

            def to_channels(src, g):
                for t in range(TG):
                    ins = e.transpose(py[:, t * P:(t + 1) * P], src[:, tile(g, t)], idf[:, :])
                ins.then_inc(s_xnT, 1)

            def gate_logits(l, g, src):
                if g + l > 0:
                    e.wait_ge(s_lgout, g + l * GROUPS)
                for t in range(TG):
                    ins = e.matmul(po[:, t * NE:(t + 1) * NE], src[:, tile(g, t)] if l == 0 else
                                   src[:, t * P:(t + 1) * P], gate[:, l, :], start=True, stop=True)
                ins.then_inc(s_lg, 1)

            def ranks(l):
                e.wait_ge(s_mask, l + 1)
                e.matmul(pb[:, 0, 0:TILES * NE], upper[:, :], mask[:, :], start=True, stop=True)
                e.matmul(pb[:, 1, 0:TILES * NE], ones[:, :], mask[:, :], start=True, stop=True).then_inc(s_rank, 1)

            e.wait_ge(s_xn, 1)
            to_channels(work_all, 0)
            for g in range(GROUPS):
                e.wait_ge(s_xT, g + 1)
                if g > 0:
                    e.wait_ge(s_lowout, g)
                e.matmul(pb[0:RANK, 3, :], wdt[:, :], xT[:, group(g)], start=True, stop=True).then_inc(s_low, 1)
                if g > 0:
                    e.wait_ge(s_parts, g)
                e.matmul(pb[0:96, 2, :], wbc[:, :], xT[:, group(g)], start=True, stop=True).then_inc(s_bc, 1)
                gate_logits(0, g, xT)
                if g + 1 < GROUPS:
                    e.wait_ge(s_xn, g + 2)
                    to_channels(work_all, g + 1)
                e.wait_ge(s_lowout, g + 1)
                e.wait_ge(s_delta, g + 1)
                e.matmul(ph[:, :], wdp[:, :], low, start=True, stop=True).then_inc(s_pre, 1)
            ranks(0)
            e.wait_ge(s_slot, 1)

            def spread(g, n, bank, ready, c):
                e.matmul(pb[:, bank, :], pick[:, c + n:c + n + 1].to_broadcast([96, P]), parts[0:96, group(g)],
                         start=True, stop=True).then_inc(ready, 1)

            def b_row(g, n):
                if 2 <= n < 4:
                    e.wait_ge(s_bx, g * NS + (n - 1))
                spread(g, n, n % 2, s_bb, 0)

            def c_row(g, n):
                if n >= 2:
                    e.wait_ge(s_prod, g * NS + (n - 1))
                spread(g, n, 2 + n % 2, s_cb, NS)

            def y_sum(g, n):
                if n >= NS - 2:
                    e.wait_ge(s_prod, g * NS + (n + 1))
                if n == 0:
                    e.wait_ge(s_att, g + 1)
                e.matmul(py[:, :], idf[:, :], work[:, 4 + n % 2, :], start=(n == 0), stop=(n == NS - 1))\
                    .then_inc(s_ysum, 1)

            def block_turn(l, g, j):
                e.wait_ge(s_row[j % XR], turn(l, g, j) * 16 + 16)
                for k in range(2):
                    ins = e.transpose(px[:, k * D:(k + 1) * D], xrow[:, j % XR, k * D:(k + 1) * D], idh[:, :])
                ins.then_inc(s_xr, 1)

            block_expert = {}

            def block_up(l, g, j):
                en = block_expert[j] = expert(e, g, j)
                e.wait_ge(s_xrout, blockno(l, g, j) + 2)
                e.wait_ge(s_gelu, blockno(l, g, j) + 1)
                xh, xl = xrT[:, j % 2, 0:D], xrT[:, j % 2, D:2 * D]
                for c in range(HC):
                    at = bass.ds(en * HID + (l * NE * HID + c * P), P)
                    o = ph[:, c * P:(c + 1) * P]
                    e.matmul(o, w1h[:, at], xh, start=True, stop=False)
                    e.matmul(o, w1h[:, at], xl, start=False, stop=False)
                    ins = e.matmul(o, w1l[:, at], xh, start=False, stop=True)
                ins.then_inc(s_l1, 1)

            def block_down(l, g, j):
                en = block_expert[j]
                e.wait_ge(s_hl, blockno(l, g, j) + 3)
                e.wait_ge(s_res, blockno(l, g, j) + 1)
                for c in range(HC):
                    at = bass.ds(en * HID + (l * NE * HID + c * P), P)
                    hh, hl = hid_h[:, j % 2, c * P:(c + 1) * P], hid_l[:, j % 2, c * P:(c + 1) * P]
                    e.matmul(po[:, 0:D], hh, w2h[:, at], start=(c == 0), stop=False)
                    e.matmul(po[:, 0:D], hh, w2l[:, at], start=False, stop=False)
                    ins = e.matmul(po[:, 0:D], hl, w2h[:, at], start=False, stop=(c == HC - 1))
                ins.then_inc(s_l2, 1)

            def blocks_at(l, g, i):
                if 1 <= i < 1 + BPG:
                    block_up(l, g, i - 1)
                if i < BPG:
                    block_turn(l, g, i)
                if 3 <= i < 3 + BPG:
                    block_down(l, g, i - 3)

            def scan_group(g, with_blocks):
                b_row(g, 0)
                b_row(g, 1)
                for n in range(NS):
                    c_row(g, n)
                    if n + 2 < NS:
                        b_row(g, n + 2)
                    if n >= 2:
                        y_sum(g, n - 2)
                    if with_blocks:
                        blocks_at(0, g, n)
                y_sum(g, NS - 2)
                y_sum(g, NS - 1)
                e.wait_ge(s_yT, g + 1)
                for t in range(TG):
                    ins = e.transpose(py[:, t * P:(t + 1) * P], yT[:, t * P:(t + 1) * P], idf[:, :])
                ins.then_inc(s_yTT, 1)

            with e.Fori(0, FIRST) as g:
                scan_group(g, False)
            with e.Fori(FIRST, GROUPS) as g:
                scan_group(g, True)

            for g in range(GROUPS):
                e.wait_ge(s_xn, g + (GROUPS + 1))
                e.wait_ge(s_xT, g + GROUPS)
                to_channels(work_all, g)
            for g in range(GROUPS):
                e.wait_ge(s_gb, g + 1)
                e.wait_ge(s_xT, g + 2 * GROUPS)
                to_channels(big, g)
                e.wait_ge(s_xT, g + (2 * GROUPS + 1))
                gate_logits(1, g, tmp_a)
            ranks(1)
            e.wait_ge(s_slot, 2)

            e.wait_ge(s_late, 48)

            def head_products(g):
                e.wait_ge(s_qks, g * 2 + 1)
                e.wait_ge(s_v, g + 1)
                e.wait_ge(s_xg, g + 1)
                for t in range(TG):
                    ins = e.matmul(pb[:, t, 0:3 * D], xTg[:, t * P:(t + 1) * P], wqkv[:, :], start=True, stop=True)
                ins.then_inc(s_qkv, 1)

            def head_sum(g):
                e.wait_ge(s_p1, g + 1)
                o = py[:, 0:TG * HD * HD].rearrange("p (t c) -> p t c", t=TG)
                for h in range(HEADS):
                    ins = e.matmul(o, idf[:, :], product[:, 0, :, h * HD * HD:(h + 1) * HD * HD],
                                   start=(h == 0), stop=(h == HEADS - 1))
                ins.then_inc(s_tsum, 1)

            with e.Fori(0, FIRST) as g:
                head_products(g)
                head_sum(g)
            with e.Fori(FIRST, GROUPS) as g:
                head_products(g)
                for i in range(BPG + 3):
                    blocks_at(1, g, i)
                    if i == 7:
                        head_sum(g)

        @block.vector
        def _(e):
            st = Steps(e, s_dve)
            hold = hold_of(e, s_held[2])
            e.sem_inc(s_scan, NS)
            e.sem_inc(s_x1, 2)
            e.sem_inc(s_hl, 2)
            for free in (s_delta, s_res, s_att, s_qks):
                e.sem_inc(free, 1)

            def stats_of(src, g):
                for t in range(TG):
                    ins = e.bn_stats(stats[:, bass.ds(g * TG + t, 1), :].rearrange("p a c -> p (a c)"),
                                     src[:, tile(g, t)])
                return ins

            def moments(n):
                m_even, q_even, m_odd, q_odd = (stats[:, :, i] for i in (1, 2, 4, 5))
                e.tensor_tensor(mean[:, :], m_even, m_odd, ALU.add)
                st.seq(e.tensor_tensor(ntmp[:, :], m_even, m_odd, ALU.subtract))
                st.seq(e.tensor_tensor(ntmp[:, :], ntmp[:, :], ntmp[:, :], ALU.mult))
                st.seq(e.tensor_tensor(vare[:, :], q_even, q_odd, ALU.add))
                e.tensor_scalar(mean[:, :], mean[:, :], 0.5, None, ALU.mult)
                st.seq(e.tensor_scalar(vare[:, :], vare[:, :], 1.0 / D, LN_EPS, ALU.mult, ALU.add))
                e.scalar_tensor_tensor(out=vare[:, :], in0=ntmp[:, :], scalar=0.25, in1=vare[:, :],
                                       op0=ALU.mult, op1=ALU.add).then_inc(s_var, 1)
                e.wait_ge(s_rstd, n)
                st.seq(e.tensor_tensor(ntmp[:, :], rstd[:, :], rstd[:, :], ALU.mult))
                st.seq(e.tensor_tensor(ntmp[:, :], ntmp[:, :], vare[:, :], ALU.mult))
                st.seq(e.tensor_scalar(ntmp[:, :], ntmp[:, :], -0.5, 1.5, ALU.mult, ALU.add))
                st.seq(e.tensor_tensor(rstd[:, :], rstd[:, :], ntmp[:, :], ALU.mult))

            def normalise(dst, src, g):
                for t in range(TG):
                    ins = e.tensor_scalar(dst[:, tile(g, t)], src[:, tile(g, t)],
                                          mean[:, col(g * TG + t)],
                                          rstd[:, col(g * TG + t)], ALU.subtract, ALU.mult)
                return ins

            def route(l):
                full, scratch = [P, TILES, NE], [0]

                def place(n):
                    scratch[0] += n
                    return work_all[:, scratch[0] - n:scratch[0]]

                def tk(v):
                    return v.rearrange("p (t k) -> p t k", t=TILES)

                top, topi = tk(place(256)), tk(place(256).bitcast(U32))
                two, first, second, spare = tk(place(64)), tk(place(256)), tk(place(256)), tk(place(256))
                totals, upto, dest = tk(place(256)), tk(place(256)), tk(place(256))
                over, per, ends, base = (place(n) for n in (NE * TILES, NE, NE, NE))
                hits, hit = place(BLOCKS * NE), place(BLOCKS)
                slotf = place(2 * TILES).rearrange("p (k t) -> p k t", k=2)
                sums, second_e = place(TILES), place(TILES)
                for t in range(TILES):
                    ins = e.max(top[:, t, :], logits[:, t, :])
                st.seq(ins)
                for t in range(TILES):
                    ins = e.max_index(topi[:, t, :], top[:, t, :], logits[:, t, :])
                st.seq(ins)
                st.seq(e.tensor_copy(two, topi[:, :, 0:2]))
                number = count[:, 0:NE].unsqueeze(1).to_broadcast(full)
                e.tensor_tensor(first, number, two[:, :, 0:1].to_broadcast(full), ALU.is_equal)
                st.seq(e.tensor_tensor(second, number, two[:, :, 1:2].to_broadcast(full), ALU.is_equal))
                e.tensor_tensor(tk(mask[:, :]), first, second, ALU.add).then_inc(s_mask, 1)
                e.tensor_tensor(logits[:, :, :], logits[:, :, :], top[:, :, 0:1].to_broadcast(full),
                                ALU.subtract).then_inc(s_expin, 1)
                e.wait_ge(s_rank, l + 1)
                rank, tot = tk(pb[:, 0, 0:TILES * NE]), tk(pb[:, 1, 0:TILES * NE])
                st.seq(e.tensor_copy(totals, tot))
                for n in range(NE):
                    ins = e.tensor_tensor_scan(upto[:, :, n], ones[:, 0:TILES], totals[:, :, n], 0.0, ALU.mult, ALU.add)
                st.seq(ins)
                st.seq(e.tensor_scalar(base, upto[:, TILES - 1, :], 1.0 / P, None, ALU.mult))
                over3 = over.rearrange("p (k j) -> p k j", k=NE)
                st.seq(e.tensor_tensor(over3, base.unsqueeze(2).to_broadcast([P, NE, TILES]),
                                       count[:, 0:TILES].unsqueeze(1).to_broadcast([P, NE, TILES]), ALU.is_gt))
                st.seq(e.tensor_reduce(per, over3, AX_X, ALU.add))
                st.seq(e.tensor_tensor_scan(ends, ones[:, 0:NE], per, 0.0, ALU.mult, ALU.add))
                st.seq(e.tensor_tensor(base, ends, per, ALU.subtract))
                st.seq(e.tensor_scalar(base, base, float(P), None, ALU.mult))
                st.seq(e.tensor_tensor(dest, rank, upto, ALU.add))
                st.seq(e.tensor_tensor(dest, dest, totals, ALU.subtract))
                st.seq(e.tensor_tensor(dest, dest, base.unsqueeze(1).to_broadcast(full), ALU.add))
                for k, chosen in enumerate((first, second)):
                    st.seq(e.tensor_tensor(spare, chosen, dest, ALU.mult))
                    st.seq(e.tensor_reduce(slotf[:, k, :], spare, AX_X, ALU.add))
                st.seq(e.tensor_copy(slot[:, :, :], slotf))
                hits3 = hits[0:1, :].rearrange("p (b k) -> p b k", b=BLOCKS)
                st.seq(e.tensor_tensor(hits3, count[0:1, :].unsqueeze(2).to_broadcast([1, BLOCKS, NE]),
                                       ends[0:1, :].unsqueeze(1).to_broadcast([1, BLOCKS, NE]), ALU.is_ge))
                st.seq(e.tensor_reduce(hit[0:1, :], hits3, AX_X, ALU.add))
                e.tensor_scalar(eid[:, :], hit[0:1, :], float(NE - 1), None, ALU.min).then_inc(s_slot, 1)
                e.wait_ge(s_expout, l + 1)
                e.tensor_reduce(sums, logits[:, :, :], AX_X, ALU.add)
                st.seq(e.tensor_tensor(spare, second, logits[:, :, :], ALU.mult))
                st.seq(e.tensor_reduce(second_e, spare, AX_X, ALU.add))
                st.seq(e.scalar_tensor_tensor(out=sums, in0=sums, scalar=TOP_EPS[l], in1=second_e,
                                              op0=ALU.mult, op1=ALU.add))
                st.seq(e.tensor_scalar(sums, sums, 1.0, None, ALU.add))
                st.seq(e.reciprocal(topw[:, 0, :], sums))
                e.tensor_tensor(topw[:, 1, :], topw[:, 0, :], second_e, ALU.mult).then_inc(s_topw, 1)
                e.wait_ge(s_topw, l + 1)

            def combine(l, pair, par):
                g = pair * 2 + par
                e.wait_ge(s_back[par], pair * 32 + (32 + l * 16 * GROUPS))
                for k in range(2):
                    for t in range(TG):
                        at = x_all[:, tile(g, t)]
                        ins = e.scalar_tensor_tensor(out=at, in0=decay[:, 2 * par + k, t * D:(t + 1) * D],
                                                     scalar=topw[:, k, col(g * TG + t)], in1=at,
                                                     op0=ALU.mult, op1=ALU.add)
                    if k == 0:
                        st.seq(ins)
                ins.then_inc(s_x1, 1)
                e.wait_ge(s_x1, g + (3 + l * GROUPS))

            e.wait_ge(s_x, 16)
            with st.loop(0, GROUPS, 1) as g:
                st.done(stats_of(x_all, g))
            st.wait()
            moments(1)
            e.wait_ge(s_const, 1)
            st.seq(e.tensor_copy(count[:, :], count_i[:, :]))
            e.wait_ge(s_aexp, 1)
            e.tensor_scalar(avec[:, :], avec[:, :], -1.0, None, ALU.mult).then_inc(s_avec, 1)

            def scan_input(g):
                e.wait_ge(s_lg, g + 1)
                hold()
                e.tensor_copy(logits[:, bass.ds(g * TG, TG), :],
                              po[:, 0:TG * NE].rearrange("p (t k) -> p t k", t=TG)).then_inc(s_lgout, 1)
                e.wait_ge(s_bc, g + 1)
                hold()
                pg, left = parts[0:96, group(g)], hid[0:96, 0, :]
                st.seq(e.tensor_copy(pg, pb[0:96, 2, :]))
                e.tensor_tensor(left, pb[0:96, 2, :], pg, ALU.subtract).then_inc(s_parts, 1)
                e.wait_ge(s_parts, g + 1)
                hold()
                e.tensor_copy(parts[32:64, group(g)], hid[32:64, 0, :])
                st.seq(e.tensor_copy(parts[64:96, group(g)], hid[64:96, 0, :]))
                st.seq(e.tensor_tensor(hid[64:96, 0, :], hid[64:96, 0, :], parts[64:96, group(g)], ALU.subtract))
                hold()
                st.seq(e.tensor_copy(parts[64:96, group(g)], hid[64:96, 0, :]))
                e.wait_ge(s_soft, g + 1)
                st.seq(e.tensor_scalar(big[:, group(g)], ph[:, :], cols[:, 0:1], 0.0, ALU.add, ALU.max))
                e.tensor_tensor(big[:, group(g)], big[:, group(g)], tmp_b[:, :], ALU.add).then_inc(s_delta, 1)
                st.seq(e.engine_nop())

            AHEAD = 2
            for g in range(AHEAD):
                normalise(work_all, x_all, g).then_inc(s_xn, 1)
            with st.loop(0, GROUPS - AHEAD, 6) as g:
                normalise(work_all, x_all, g + AHEAD).then_inc(s_xn, 1)
                scan_input(g)
            for g in range(GROUPS - AHEAD, GROUPS):
                scan_input(g)
            e.wait_ge(s_rlo, GROUPS)
            route(0)

            def block_split(l, g, j):
                e.wait_ge(s_gelu, blockno(l, g, j) + 2)
                st.seq(e.tensor_copy(hid_h[:, j % 2, :], hid[:, j % 2, :]))
                e.tensor_tensor(hid_l[:, j % 2, :], hid[:, j % 2, :], hid_h[:, j % 2, :], ALU.subtract).then_inc(s_hl, 1)

            def block_out(l, g, j):
                en = expert(e, g, j)
                e.wait_ge(s_l2, blockno(l, g, j) + 1)
                e.tensor_tensor(res[:, j % XR, :], po[:, 0:D], b2[:, bass.ds(en * D, D)], ALU.add).then_inc(s_res, 1)

            def blocks_at(l, g, i):
                if 4 <= i < 4 + BPG:
                    block_out(l, g, i - 4)
                if 2 <= i < 2 + BPG:
                    block_split(l, g, i - 2)

            def scan_group(g, with_blocks):
                dx = work[:, 6, :]
                st.seq(e.tensor_tensor(dx, big[:, group(g)], xT[:, group(g)], ALU.mult))

                def drive(n):
                    e.wait_ge(s_bb, g * NS + (n + 1))
                    if n >= 2:
                        e.wait_ge(s_scan, g * NS + (n - 1 + NS))
                    e.tensor_tensor(work[:, n % 2, :], dx, pb[:, n % 2, :], ALU.mult).then_inc(s_bx, 1)

                def scan(n):
                    e.wait_ge(s_a, g * NS + (n + 1))
                    e.wait_ge(s_bx, g * NS + (n + 1))
                    if n >= 2:
                        e.wait_ge(s_prod, g * NS + (n - 1))
                    for h in range(GC // SLEN):
                        sl = slice(h * SLEN, (h + 1) * SLEN)
                        ins = e.tensor_tensor_scan(work[:, 2 + n % 2, sl], decay[:, n, sl], work[:, n % 2, sl],
                                                   0.0, ALU.mult, ALU.add)
                    ins.then_inc(s_scan, 1)

                def weigh(n):
                    e.wait_ge(s_cb, g * NS + (n + 1))
                    e.wait_ge(s_scan, g * NS + (n + 1 + NS))
                    if n >= 2:
                        e.wait_ge(s_ysum, g * NS + (n - 1))
                    e.tensor_tensor(work[:, 4 + n % 2, :], work[:, 2 + n % 2, :], pb[:, 2 + n % 2, :],
                                    ALU.mult).then_inc(s_prod, 1)

                drive(0)
                for n in range(NS):
                    if n + 1 < NS:
                        drive(n + 1)
                    scan(n)
                    if n >= 1:
                        weigh(n - 1)
                    if with_blocks:
                        blocks_at(0, g, n)
                weigh(NS - 1)
                e.wait_ge(s_ysum, g * NS + NS)
                e.scalar_tensor_tensor(out=yT, in0=xT[:, group(g)], scalar=cols[:, 1:2], in1=py[:, :],
                                       op0=ALU.mult, op1=ALU.add).then_inc(s_yT, 1)
                e.wait_ge(s_yTT, g + 1)
                e.tensor_tensor(x_all[:, group(g)], x_all[:, group(g)], py[:, :], ALU.add).then_inc(s_att, 1)

            with st.loop(0, FIRST, 1) as g:
                scan_group(g, False)
            e.wait_ge(s_b2, 16)
            with st.loop(FIRST, GROUPS, 1 + BPG) as g:
                scan_group(g, True)

            with st.loop(0, GROUPS // 2, 4) as pair:
                for par in range(2):
                    combine(0, pair, par)
                    st.done(stats_of(x_all, pair * 2 + par))
            st.wait()
            moments(2)
            with st.loop(0, GROUPS, 1) as g:
                normalise(work_all, x_all, g).then_inc(s_xn, 1)
                e.wait_ge(s_xn, g + (GROUPS + 1))
                st.done(stats_of(work_all, g))
            st.wait()
            moments(3)
            with e.Fori(0, GROUPS) as g:
                normalise(big, work_all, g).then_inc(s_xf, 1)
            with e.Fori(0, GROUPS) as g:
                e.wait_ge(s_lg, g + (GROUPS + 1))
                e.tensor_tensor(logits[:, bass.ds(g * TG, TG), :],
                                po[:, 0:TG * NE].rearrange("p (t k) -> p t k", t=TG),
                                bgate[:, :].unsqueeze(1).to_broadcast([P, TG, NE]), ALU.add).then_inc(s_lgout, 1)
            e.wait_ge(s_lgout, 2 * GROUPS)
            e.wait_ge(s_add, GROUPS)
            route(1)

            q_, k_, v_, t_, o_ = (work[:, i, :] for i in range(5))
            qmax, kmax, qsum, ksum = (work[:, 5, i * 64:i * 64 + n] for i, n in enumerate((64, 32, 64, 32)))

            def heads_at(g, i):
                psq = pb[:, :, 0:D].rearrange("p t (h d) -> p t h d", d=HD)
                psk = pb[:, :, D:2 * D].rearrange("p t (h d) -> p t d h", d=HD)
                if i == 0:
                    e.wait_ge(s_v, g + 2)
                    e.tensor_reduce(qmax.rearrange("p (t h) -> p t h", t=TG), psq, AX_X, ALU.max)
                    st.seq(e.tensor_reduce(kmax.rearrange("p (t d) -> p t d", t=TG), psk, AX_X, ALU.max))
                    e.tensor_tensor(q_.rearrange("p (t h d) -> p t h d", t=TG, d=HD), psq,
                                    qmax.rearrange("p (t h) -> p t h", t=TG).unsqueeze(3).to_broadcast(
                                        [P, TG, HEADS, HD]), ALU.subtract).then_inc(s_qks, 1)
                    e.tensor_tensor(k_.rearrange("p (t h d) -> p t h d", t=TG, d=HD),
                                    pb[:, :, D:2 * D].rearrange("p t (h d) -> p t h d", d=HD),
                                    kmax.rearrange("p (t d) -> p t d", t=TG).unsqueeze(2).to_broadcast(
                                        [P, TG, HEADS, HD]), ALU.subtract).then_inc(s_qks, 1)
                if i == 1:
                    e.wait_ge(s_qke, g * 2 + 2)
                    e.tensor_reduce(qsum, q_.rearrange("p (c d) -> p c d", d=HD), AX_X, ALU.add)
                    st.seq(e.tensor_reduce(ksum.rearrange("p (t d) -> p t d", t=TG),
                                           k_.rearrange("p (t h d) -> p t d h", t=TG, d=HD), AX_X, ALU.add))
                    e.reciprocal(qsum, qsum)
                    st.seq(e.reciprocal(ksum, ksum))
                if 2 <= i < 2 + TG:
                    t = i - 2
                    full = [P, HEADS, HD, HD]
                    kt = k_[:, t * D:(t + 1) * D].rearrange("p (h d) -> p h d", d=HD).unsqueeze(3).to_broadcast(full)
                    vt = v_[:, t * D:(t + 1) * D].rearrange("p (h d) -> p h d", d=HD).unsqueeze(2).to_broadcast(full)
                    ins = e.tensor_tensor(product[:, 0, t, :].rearrange("p (h d c) -> p h d c", d=HD, c=HD),
                                          kt, vt, ALU.mult)
                    if t == TG - 1:
                        ins.then_inc(s_p1, 1)
                if i == 8:
                    e.wait_ge(s_tsum, g + 1)
                    st.seq(e.tensor_tensor(t_[:, 0:TG * HD * HD].rearrange("p (c d) -> p c d", d=HD),
                                           py[:, 0:TG * HD * HD].rearrange("p (c d) -> p c d", d=HD),
                                           ksum.unsqueeze(2).to_broadcast([P, TG * HD, HD]), ALU.mult))
                if 8 <= i < 8 + TG:
                    t = i - 8
                    full = [P, HEADS, HD, HD]
                    qt = q_[:, t * D:(t + 1) * D].rearrange("p (h d) -> p h d", d=HD).unsqueeze(2).to_broadcast(full)
                    tt = t_[:, t * HD * HD:(t + 1) * HD * HD].rearrange("p (d c) -> p c d", d=HD)\
                        .unsqueeze(1).to_broadcast(full)
                    ins = e.tensor_tensor(product[:, 1, t, :].rearrange("p (h c d) -> p h c d", d=HD, c=HD),
                                          qt, tt, ALU.mult)
                    st.done(ins)
                if i == 8 + TG:
                    st.wait()
                    st.seq(e.tensor_reduce(o_, product[:, 1, :, :].rearrange("p t (c d) -> p (t c) d", d=HD),
                                           AX_X, ALU.add))
                    o3 = o_.rearrange("p (c d) -> p c d", d=HD)
                    st.seq(e.tensor_tensor(o3, o3, qsum.unsqueeze(2).to_broadcast([P, TG * HEADS, HD]), ALU.mult))
                    e.tensor_tensor(x_all[:, group(g)], x_all[:, group(g)], o_, ALU.add).then_inc(s_att, 1)

            with st.loop(0, FIRST, 10) as g:
                for i in range(8 + TG + 1):
                    heads_at(g, i)
            e.wait_ge(s_b2, 32)
            with st.loop(FIRST, GROUPS, 10 + BPG) as g:
                for i in range(4 + BPG):
                    heads_at(g, i)
                    blocks_at(1, g, i)
            with st.loop(0, GROUPS // 2, 2) as pair:
                for par in range(2):
                    combine(1, pair, par)


def kernel(**inputs):
    import numpy as np
    import concourse.bacc as bacc
    from concourse.bass_utils import run_bass_kernel_spmd

    L0, L1 = "L0_attn_", "L1_attn_"
    v = {k: np.asarray(w) for k, w in inputs.items()}

    def columns(b):
        return b.reshape(NE, HC, P).transpose(2, 0, 1).reshape(P, NE * HC)

    arrays = {
        "x": v[L0 + "x"].reshape(NTOK, D), "A_log": v[L0 + "A_log"], "D_param": v[L0 + "D_param"].reshape(D, 1),
        "W_bc": v[L0 + "W_bc"], "W_dt": v[L0 + "W_dt"], "W_dtproj": v[L0 + "W_dtproj"],
        "b_dt": v[L0 + "b_dtproj"].reshape(D, 1), "gate_0": v["L0_ffn_gate_w"].T, "gate_1": v["L1_ffn_Wg"].T,
        "w1_0": v["L0_ffn_w1"],
        "w2_0": v["L0_ffn_w2"].reshape(NE, HC, P, D).transpose(0, 2, 1, 3).reshape(NE, P, HID),
        "b1_0": columns(v["L0_ffn_b1"]), "b2_0": v["L0_ffn_b2"].reshape(1, NE * D),
        "wqkv": np.concatenate([v[L1 + "W_Q"].T, v[L1 + "W_K"].T, v[L1 + "W_V"].T], axis=1),
        "gamma": v["L1_ffn_gamma"].reshape(1, D), "beta": v["L1_ffn_beta"].reshape(1, D),
        "bg": v["L1_ffn_bg"].reshape(1, NE), "w1_1": v["L1_ffn_W1"].transpose(0, 2, 1),
        "w2_1": v["L1_ffn_W2"].reshape(NE, D, HC, P).transpose(0, 3, 2, 1).reshape(NE, P, HID),
        "b1_1": columns(v["L1_ffn_b1"]), "b2_1": v["L1_ffn_b2"].reshape(1, NE * D),
    }
    arrays = {k: np.ascontiguousarray(w) for k, w in arrays.items()}
    nc = bacc.Bacc("TRN2", target_bir_lowering=False, num_devices=1)
    aps = {k: nc.dram_tensor("in_" + k, w.shape, mybir.dt.from_np(w.dtype), kind="ExternalInput").ap()
           for k, w in arrays.items()}
    out = nc.dram_tensor("out", [NTOK, D], F32, kind="ExternalOutput").ap()
    build(nc, aps, out)
    r = run_bass_kernel_spmd(nc, [{"in_" + k: w for k, w in arrays.items()}], core_ids=[0])
    return r.results[0]["out"].reshape(SEQ, SLEN, D)
```

```python
from contextlib import ExitStack, contextmanager

import concourse.bass as bass
from concourse import mybir

ALU = mybir.AluOpType
ACT = mybir.ActivationFunctionType
AX_X = mybir.AxisListType.X
F32, F16, BF16 = mybir.dt.float32, mybir.dt.float16, mybir.dt.bfloat16
I32, U32 = mybir.dt.int32, mybir.dt.uint32

P = 128
SEQ, SLEN, D = 16, 256, 128
NTOK = SEQ * SLEN
TILES = NTOK // P
GROUPS = 8
TG = TILES // GROUPS
GC = TG * P
NS = 16
RANK = 64
NE = 8
HID = 512
HC = HID // P
HEADS, HD = 16, 8
LN_EPS = 1e-5
TOP_EPS = (1e-9, 1e-8)
BLOCKS = 72
FIRST = 2
BPG = BLOCKS // (GROUPS - FIRST)
ROWF = 2 * D + 2
STEPS = 16
BACK = 4
XR = 6
assert BLOCKS >= 2 * TILES + NE - 1 and BPG % XR == 0 and BPG + 4 <= STEPS


class Steps:

    def __init__(self, eng, sem):
        self.eng, self.sem, self.n, self.off = eng, sem, 0, 0

    def done(self, ins):
        ins.then_inc(self.sem, 1)
        self.n += 1

    def wait(self):
        self.eng.wait_ge(self.sem, self.off + self.n)

    def seq(self, ins):
        self.done(ins)
        self.wait()

    @contextmanager
    def loop(self, first, end, per):
        n0 = self.n
        with self.eng.Fori(first, end) as i:
            self.off = (i - first) * per
            yield i
        assert self.n == n0 + per, (self.n - n0, per)
        self.n, self.off = n0 + per * (end - first), 0


def hold_of(eng, held):
    return lambda: eng.sem_inc(held, 1)


def build(nc, a, out):
    ctx = ExitStack()
    with ctx:
        def sb(name, shape, dt=F32):
            return ctx.enter_context(nc.sbuf_tensor(name, shape, dt))

        def ps(name, shape, dt=F32):
            return ctx.enter_context(nc.psum_tensor(name, shape, dt))

        def sem(name):
            return ctx.enter_context(nc.semaphore(name))

        def dram(name, shape, dt):
            return nc.dram_tensor(name, shape, dt, kind="Internal").ap()

        slots_dram = [dram(f"slots{l}", [BLOCKS * P, ROWF], F16) for l in range(2)]
        NRES = 2 * NTOK
        res_dram = [dram(f"results{l}", [NRES, D], F32) for l in range(2)]

        x = sb("x", [P, TILES, D])
        xT = sb("xT", [P, NTOK])
        big = sb("big", [P, NTOK])
        parts = sb("parts", [P, NTOK], BF16)
        rows = sb("rows", [P, TILES, ROWF], F16)
        decay = sb("decay", [P, NS, GC])
        work = sb("work", [P, 8, GC])
        w1h = sb("w1h", [P, 2 * NE * HID], F16)
        w1l = sb("w1l", [P, 2 * NE * HID], F16)
        w2h = sb("w2h", [P, 2 * NE * HID], F16)
        w2l = sb("w2l", [P, 2 * NE * HID], F16)
        xrow = sb("xrow", [P, XR, ROWF], F16)
        xrT = sb("xrT", [P, 2, 2 * D], F16)
        hid = sb("hid", [P, 2, HID])
        hid_h = sb("hid_h", [P, 2, HID], F16)
        hid_l = sb("hid_l", [P, 2, HID], F16)
        res = sb("res", [P, XR, D])
        b1 = sb("b1", [P, 2 * NE * HC])
        idf = sb("idf", [P, P])
        idh = sb("idh", [P, P], F16)
        upper = sb("upper", [P, P], BF16)
        ones = sb("ones", [P, P], BF16)
        pick = sb("pick", [96, 2 * NS], BF16)
        wbc = sb("wbc", [P, 96])
        wdt = sb("wdt", [P, RANK])
        wdp = sb("wdp", [RANK, D])
        gate = sb("gate", [P, 2, NE])
        cols = sb("cols", [P, 2 + NS])
        avec = sb("avec", [P, NS])
        bgate = sb("bgate", [P, NE])
        stats = sb("stats", [P, TILES, 6])
        mean = sb("mean", [P, TILES])
        vare = sb("vare", [P, TILES])
        rstd = sb("rstd", [P, TILES])
        ntmp = sb("ntmp", [P, TILES])
        logits = sb("logits", [P, TILES, NE])
        mask = sb("mask", [P, TILES * NE], BF16)
        count_i = sb("count_i", [P, BLOCKS], I32)
        count = sb("count", [P, BLOCKS])
        topw = sb("topw", [P, 2, TILES])
        slot = sb("slot", [P, 2, TILES], I32)
        eid = sb("eid", [1, BLOCKS], I32)

        pb = ps("pb", [P, 4, GC])
        py = ps("py", [P, GC])
        px = ps("px", [P, 2 * D], F16)
        ph = ps("ph", [P, HID])
        po = ps("po", [P, GC])

        s_x = sem("s_x")
        s_small = sem("s_small")
        s_late = sem("s_late")
        s_b2 = sem("s_b2")
        s_stage = [sem(f"s_stage{i}") for i in range(8)]
        s_zeroed = [sem(f"s_zeroed{l}") for l in range(2)]
        s_disp = [sem(f"s_disp{l}") for l in range(2)]
        s_row = [sem(f"s_row{i}") for i in range(XR)]
        s_sent = [sem(f"s_sent{i}") for i in range(XR)]
        s_back = [sem(f"s_back{i}") for i in range(BACK)]
        s_out = sem("s_out")
        s_pool = sem("s_pool")
        s_act = sem("s_act")
        s_dve = sem("s_dve")
        s_const = sem("s_const")
        s_ones = sem("s_ones")
        s_held = [sem(f"s_held{i}") for i in range(3)]
        s_aexp = sem("s_aexp")
        s_avec = sem("s_avec")
        s_whi, s_wlo = sem("s_whi"), sem("s_wlo")
        s_var, s_rstd = sem("s_var"), sem("s_rstd")
        s_xn = sem("s_xn")
        s_xnT = sem("s_xnT")
        s_xT = sem("s_xT")
        s_lg = sem("s_lg")
        s_bc, s_parts = sem("s_bc"), sem("s_parts")
        s_low, s_lowout = sem("s_low"), sem("s_lowout")
        s_pre = sem("s_pre")
        s_soft = sem("s_soft")
        s_delta = sem("s_delta")
        s_rhi = sem("s_rhi")
        s_rlo = sem("s_rlo")
        s_mask, s_rank = sem("s_mask"), sem("s_rank")
        s_expin, s_expout = sem("s_expin"), sem("s_expout")
        s_topw = sem("s_topw")
        s_slot = sem("s_slot")
        s_bb, s_cb = sem("s_bb"), sem("s_cb")
        s_bx = sem("s_bx")
        s_a = sem("s_a")
        s_scan = sem("s_scan")
        s_prod = sem("s_prod")
        s_ysum = sem("s_ysum")
        s_yT, s_yTT = sem("s_yT"), sem("s_yTT")
        s_att = sem("s_att")
        s_xr, s_xrout = sem("s_xr"), sem("s_xrout")
        s_l1, s_gelu, s_hl = sem("s_l1"), sem("s_gelu"), sem("s_hl")
        s_l2, s_res = sem("s_l2"), sem("s_res")
        s_x1 = sem("s_x1")
        s_add = sem("s_add")
        s_norm = sem("s_norm")
        s_xf, s_gb = sem("s_xf"), sem("s_gb")
        s_xg = sem("s_xg")
        s_qkv, s_v = sem("s_qkv"), sem("s_v")
        s_qks, s_qke = sem("s_qks"), sem("s_qke")
        s_tran = sem("s_tran")
        s_p1, s_tsum = sem("s_p1"), sem("s_tsum")
        block = ctx.enter_context(nc.Block())

        decay_all = decay[:, :, :].rearrange("p a c -> p (a c)")
        stage = decay_all.rearrange("p (s c) -> p s c", s=8)
        rows_id = rows[:, :, :].rearrange("p t c -> p (t c)").bitcast(I32).rearrange(
            "p (t c) -> p t c", t=TILES)[:, :, D]
        b2 = rows[:, :, :].rearrange("p t c -> p (t c)").bitcast(F32)[:, 0:NE * D]
        parts_f = parts[:, :].bitcast(F32)
        wqkv = parts_f[:, 0:3 * D]
        gb = parts_f[:, 3 * D:5 * D].rearrange("p (k d) -> p k d", k=2)
        fill = xrow[:, 0, :]
        tmp_a = hid_h[:, :, :].rearrange("p r c -> p (r c)").bitcast(F32)
        tmp_b = hid_l[:, :, :].rearrange("p r c -> p (r c)").bitcast(F32)
        yT = work[:, 7, :]
        xTg = work[:, 6, :]
        fill_id = fill[:, :].bitcast(I32)[:, D:D + 1]
        work_all = work[:, :, :].rearrange("p a c -> p (a c)")
        xn = work_all.rearrange("p (t c) -> p t c", c=D)
        x_all = x[:, :, :].rearrange("p t c -> p (t c)")
        xf = big[:, :].rearrange("p (t c) -> p t c", t=TILES)
        logits_all = logits[:, :, :].rearrange("p t k -> p (t k)")
        low = res[:, :, :].rearrange("p r c -> p (r c)")[0:RANK, 0:GC]
        product = decay_all.rearrange("p (k t c) -> p k t c", k=2, t=TG)
        SMALL = 13

        def ids_of(r):
            return xrow[:, r, :].bitcast(I32)[:, D:D + 1]

        def group(g):
            return bass.ds(g * GC, GC)

        def tile(g, t):
            return bass.ds(g * GC + t * P, P)

        def col(i):
            return bass.ds(i, 1)

        def blockno(l, g, j):
            return (g - FIRST) * BPG + (j + l * BLOCKS)

        def turn(l, g, j):
            return (g - FIRST) * (BPG // XR) + (j // XR + l * (BLOCKS // XR))

        def turned(par):
            return ph[:, :] if par else py[:, :]

        def xfT(par):
            return tmp_b[:, :] if par else tmp_a[:, :]

        def hidden(l, j):
            return py if l == 1 and j % 2 else ph

        def expert(e, g, j):
            return e.value_load(eid[0:1, col((g - FIRST) * BPG + j)], min_val=0, max_val=NE - 1)

        @block.sync
        def _(e):
            e.dma_start(x[:, :, :], a["x"].rearrange("(t p) d -> p t d", p=P)).then_inc(s_x, 16)
            small = [(wbc[:, 32 * q:32 * q + 32], a["W_bc"]) for q in range(3)]
            small += [(wdt[:, :], a["W_dt"]), (wdp[:, :], a["W_dtproj"]), (gate[:, 0, :], a["gate_0"]),
                      (gate[:, 1, :], a["gate_1"]), (cols[:, 0:1], a["b_dt"]),
                      (cols[:, 1:2], a["D_param"]), (cols[:, 2:2 + NS], a["A_log"]),
                      (b1[:, 0:NE * HC], a["b1_0"]), (b1[:, NE * HC:2 * NE * HC], a["b1_1"]),
                      (bgate[:, :], a["bg"].to_broadcast([P, NE]))]
            assert len(small) == SMALL
            for dst, src in small:
                e.dma_start(dst, src).then_inc(s_small, 16)
            for i in range(2 * NE):
                l, n = i // NE, i % NE
                if i >= 8:
                    e.wait_ge(s_wlo, i - 7)
                e.dma_start(stage[:, i % 8, 0:HID], a[f"w1_{l}"][n]).then_inc(s_stage[i % 8], 16)
                e.dma_start(stage[:, i % 8, HID:2 * HID], a[f"w2_{l}"][n]).then_inc(s_stage[i % 8], 16)
            e.wait_ge(s_const, 1)
            for l in range(2):
                e.dma_start(slots_dram[l].rearrange("(b p) c -> p b c", p=P),
                            fill[:, :].unsqueeze(1).to_broadcast([P, BLOCKS, ROWF])).then_inc(s_zeroed[l], 16)

            for l in range(2):
                e.wait_ge(s_disp[l], 16 * 2 * TILES)
                e.dma_start(b2, a[f"b2_{l}"].to_broadcast([P, NE * D])).then_inc(s_b2, 16)

                def block_rows(g, j, used):
                    if used:
                        e.wait_ge(s_sent[j % XR], turn(l, g, j) * 16)
                    e.dma_start(xrow[:, j % XR, :], slots_dram[l][bass.ds(blockno(0, g, j) * P, P), :])\
                        .then_inc(s_row[j % XR], 16)

                for j in range(BPG):
                    block_rows(FIRST, j, l * BPG + j >= XR)
                with e.Fori(FIRST + 1, GROUPS) as g:
                    for j in range(BPG):
                        block_rows(g, j, True)
                for r in range(XR):
                    e.wait_ge(s_sent[r], 16 * (l + 1) * (BLOCKS // XR))
                e.wait_ge(s_att, (l + 1) * GROUPS + 1)
                if l == 0:
                    for dst, src in ((wqkv, a["wqkv"]), (gb[:, 0, :], a["gamma"].to_broadcast([P, D])),
                                     (gb[:, 1, :], a["beta"].to_broadcast([P, D]))):
                        e.dma_start(dst, src).then_inc(s_late, 16)
                with e.Fori(0, GROUPS // BACK) as turn_:
                    for q in range(BACK):
                        g = turn_ * BACK + q
                        e.wait_ge(s_x1, g + (1 + l * GROUPS))
                        for k in range(2):
                            e.dma_start(decay[:, 2 * q + k, :].rearrange("p (t c) -> p t c", t=TG),
                                        res_dram[l][bass.ds(g * GC + k * NTOK, GC), :].rearrange(
                                            "(t p) c -> p t c", p=P)).then_inc(s_back[q], 16)

        @block.gpsimd
        def _(e):
            st = Steps(e, s_pool)
            hold = hold_of(e, s_held[0])
            e.memset(ones[:, :], 1.0).then_inc(s_ones, 1)
            e.memset(idf[:, :], 0.0)
            e.memset(idh[:, :], 0.0)
            e.memset(upper[:, :], 1.0)
            e.memset(pick[:, :], 0.0)
            e.iota(count_i[:, :], pattern=[[1, BLOCKS]], base=0, channel_multiplier=0)
            st.seq(e.memset(fill[:, :], 0.0))
            e.affine_select(out=idf[:, :], in_=idf[:, :], compare_op=ALU.not_equal, fill=1.0, base=0,
                            pattern=[[-1, P]], channel_multiplier=1)
            e.affine_select(out=idh[:, :], in_=idh[:, :], compare_op=ALU.not_equal, fill=1.0, base=0,
                            pattern=[[-1, P]], channel_multiplier=1)
            e.affine_select(out=upper[:, :], in_=upper[:, :], compare_op=ALU.is_gt, fill=0.0, base=0,
                            pattern=[[1, P]], channel_multiplier=-1)
            e.iota(fill_id, pattern=[[0, 1]], base=NRES, channel_multiplier=0)
            for q in range(3):
                st.seq(e.affine_select(out=pick[:, :], in_=pick[:, :], compare_op=ALU.not_equal, fill=1.0,
                                       base=-32 * q, pattern=[[-1, 2 * NS]], channel_multiplier=1))
            e.memset(eid[:, :], 0).then_inc(s_const, 1)
            def rows_low(l, g):
                hi, lo = (rows[:, bass.ds(g * TG, TG), k * D:(k + 1) * D] for k in range(2))
                e.tensor_tensor(lo, (xf if l else xn)[:, bass.ds(g * TG, TG), :], hi, ALU.subtract).then_inc(s_rlo, 1)

            for i in range(2 * NE):
                if i % 2 == 0:
                    e.wait_ge(s_rhi, i // 2 + 1)
                    rows_low(0, i // 2)
                e.wait_ge(s_whi, i + 1)
                sl = slice(i * HID, (i + 1) * HID)
                e.tensor_tensor(w1l[:, sl], stage[:, i % 8, 0:HID], w1h[:, sl], ALU.subtract)
                e.tensor_tensor(w2l[:, sl], stage[:, i % 8, HID:2 * HID], w2h[:, sl], ALU.subtract).then_inc(s_wlo, 1)

            for l in range(2):
                if l == 1:
                    with e.Fori(0, GROUPS) as g:
                        e.wait_ge(s_xn, g + (GROUPS + 1))
                        hold()
                        e.tensor_tensor(x_all[:, group(g)], x_all[:, group(g)], work_all[:, group(g)],
                                        ALU.add).then_inc(s_add, 1)
                    with e.Fori(0, GROUPS) as g:
                        e.wait_ge(s_rhi, g + (GROUPS + 1))
                        hold()
                        rows_low(1, g)
                st.seq(e.iota(rows_id, pattern=[[P, TILES]], base=0, channel_multiplier=1))
                e.wait_ge(s_rlo, (l + 1) * GROUPS)
                e.wait_ge(s_zeroed[l], 16)
                e.wait_ge(s_slot, l + 1)
                for k in range(2):
                    for t in range(TILES):
                        e.indirect_dma_start(slots_dram[l], bass.IndirectOffsetOnAxis(slot[:, k, t:t + 1], 0),
                                             rows[:, t, :], None).then_inc(s_disp[l], 16)
                    if k == 0:
                        e.wait_ge(s_disp[l], 16 * TILES)
                        st.seq(e.iota(rows_id, pattern=[[P, TILES]], base=NTOK, channel_multiplier=1))
                with e.Fori(FIRST, GROUPS) as g:
                    for j in range(BPG):
                        e.wait_ge(s_res, blockno(l, g, j) + 2)
                        hold()
                        e.indirect_dma_start(res_dram[l], bass.IndirectOffsetOnAxis(ids_of(j % XR), 0),
                                             res[:, j % XR, :], None, bounds_check=NRES - 1,
                                             oob_is_err=False).then_inc(s_sent[j % XR], 16)

        @block.scalar
        def _(e):
            st = Steps(e, s_act)
            hold = hold_of(e, s_held[1])
            for free in (s_xrout, s_gelu, s_v):
                e.sem_inc(free, 1)
            e.wait_ge(s_small, 16 * SMALL)
            e.activation(avec[:, :], cols[:, 2:2 + NS], ACT.Exp).then_inc(s_aexp, 1)

            def rstd_of(n):
                e.wait_ge(s_var, n)
                st.seq(e.activation(ntmp[:, :], vare[:, :], ACT.Ln))
                e.activation(rstd[:, :], ntmp[:, :], ACT.Exp, scale=-0.5).then_inc(s_rstd, 1)

            def gate_exp(n):
                e.wait_ge(s_expin, n)
                e.activation(logits_all, logits_all, ACT.Exp).then_inc(s_expout, 1)

            rstd_of(1)

            def channels_out(g):
                e.wait_ge(s_xnT, g + 1)
                e.copy(xT[:, group(g)], py[:, :]).then_inc(s_xT, 1)

            def rows_high(l, g):
                hi = rows[:, bass.ds(g * TG, TG), 0:D]
                if l == 0:
                    e.wait_ge(s_xn, g + 1)
                    e.copy(hi, xn[:, bass.ds(g * TG, TG), :]).then_inc(s_rhi, 1)
                else:
                    e.wait_ge(s_gb, g + 1)
                    hold()
                    e.copy(hi, xf[:, bass.ds(g * TG, TG), :]).then_inc(s_rhi, 1)

            def low_out(g):
                e.wait_ge(s_low, g + 1)
                if g > 0:
                    e.wait_ge(s_pre, g)
                e.copy(low, pb[0:RANK, 3, :]).then_inc(s_lowout, 1)

            def softplus(g):
                e.wait_ge(s_pre, g + 1)
                st.seq(e.activation(tmp_a[:, :], ph[:, :], ACT.Abs, bias=cols[:, 0:1]))
                st.seq(e.activation(tmp_a[:, :], tmp_a[:, :], ACT.Exp, scale=-1.0))
                e.wait_ge(s_delta, g + 1)
                e.activation(tmp_b[:, :], tmp_a[:, :], ACT.Ln, bias=1.0).then_inc(s_soft, 1)

            def weights_high(i):
                e.wait_ge(s_stage[i % 8], 32 * (i // 8 + 1))
                sl = slice(i * HID, (i + 1) * HID)
                e.copy(w1h[:, sl], stage[:, i % 8, 0:HID])
                e.copy(w2h[:, sl], stage[:, i % 8, HID:2 * HID]).then_inc(s_whi, 1)

            channels_out(0)
            for g in range(GROUPS):
                rows_high(0, g)
                low_out(g)
                weights_high(2 * g)
                if g + 1 < GROUPS:
                    channels_out(g + 1)
                softplus(g)
                weights_high(2 * g + 1)
            gate_exp(1)

            def decay_of(g, n):
                e.wait_ge(s_scan, g * NS + (n + 1))
                hold()
                e.activation(decay[:, n, :], big[:, group(g)], ACT.Exp, scale=avec[:, n:n + 1]).then_inc(s_a, 1)

            def block_in(l, g, j):
                e.wait_ge(s_xr, blockno(l, g, j) + 1)
                e.copy(xrT[:, j % 2, :], px[:, :]).then_inc(s_xrout, 1)

            def block_gelu(l, g, j):
                en = expert(e, g, j)
                e.wait_ge(s_hl, blockno(l, g, j) + 1)
                e.wait_ge(s_l1, blockno(l, g, j) + 1)
                hold()
                for c in range(HC):
                    ins = e.activation(hid[:, j % 2, c * P:(c + 1) * P], hidden(l, j)[:, c * P:(c + 1) * P], ACT.Gelu,
                                       bias=b1[:, col(en * HC + (l * NE * HC + c))])
                ins.then_inc(s_gelu, 1)

            def blocks_at(l, g, i):
                if i < BPG:
                    block_in(l, g, i)
                if 1 <= i < 1 + BPG:
                    block_gelu(l, g, i - 1)

            def scan_group(g, with_blocks, last=False):
                if with_blocks:
                    for i in range(BPG + 1):
                        blocks_at(0, g, i)
                if not last:
                    for n in range(NS):
                        decay_of(g + 1, n)

            e.wait_ge(s_wlo, 2 * NE)
            e.wait_ge(s_avec, 1)
            for n in range(NS):
                decay_of(0, n)
            with e.Fori(0, FIRST) as g:
                scan_group(g, False)
            with e.Fori(FIRST, GROUPS - 1) as g:
                scan_group(g, True)
            scan_group(GROUPS - 1, True, last=True)

            rstd_of(2)

            def normalise(g):
                for t in range(TG):
                    ins = e.activation(work_all[:, tile(g, t)], x_all[:, tile(g, t)], ACT.Identity,
                                       bias=ntmp[:, col(g * TG + t)], scale=rstd[:, col(g * TG + t)])
                ins.then_inc(s_xn, 1)

            e.wait_ge(s_norm, 1)
            normalise(0)
            normalise(1)
            with e.Fori(0, GROUPS // 2 - 1) as pair:
                for par in range(2):
                    g = pair * 2 + par
                    e.wait_ge(s_xnT, g + (GROUPS + 1))
                    hold()
                    e.copy(xT[:, group(g)], turned(par)).then_inc(s_xT, 1)
                    normalise(g + 2)
            for g in range(GROUPS - 2, GROUPS):
                e.wait_ge(s_xnT, g + (GROUPS + 1))
                e.copy(xT[:, group(g)], turned(g % 2)).then_inc(s_xT, 1)
            rstd_of(3)
            with e.Fori(0, GROUPS // 2) as pair:
                for par in range(2):
                    g = pair * 2 + par
                    rows_high(1, g)
                    e.wait_ge(s_xnT, g + (2 * GROUPS + 1))
                    e.wait_ge(s_lg, g + (GROUPS - 1))
                    e.copy(xfT(par), turned(par)).then_inc(s_xT, 1)
            gate_exp(2)

            def head_input(g):
                e.wait_ge(s_qkv, g + 1)
                hold()
                e.copy(xTg, xT[:, group(g)]).then_inc(s_xg, 1)

            def v_out(g):
                e.wait_ge(s_qkv, g + 2)
                e.copy(work[:, 2, :].rearrange("p (t c) -> p t c", t=TG), pb[:, :, 2 * D:3 * D]).then_inc(s_v, 1)

            def head_exps(g):
                for k in range(2):
                    e.wait_ge(s_qks, g * 2 + (k + 2))
                    e.activation(work[:, k, :], work[:, k, :], ACT.Exp).then_inc(s_qke, 1)

            def head_group(g, with_blocks, last=False):
                for i in range(STEPS):
                    if with_blocks:
                        blocks_at(1, g, i)
                    if i == 0:
                        head_exps(g)
                    if i == 8 and not last:
                        head_input(g + 1)
                    if i == 13 and not last:
                        v_out(g + 1)

            e.wait_ge(s_topw, 2)
            head_input(0)
            v_out(0)
            with e.Fori(0, FIRST) as g:
                head_group(g, False)
            with e.Fori(FIRST, GROUPS - 1) as g:
                head_group(g, True)
            head_group(GROUPS - 1, True, last=True)
            with e.Fori(0, GROUPS) as g:
                e.wait_ge(s_x1, g + (GROUPS + BACK + 1))
                e.dma_start(out[bass.ds(g * GC, GC), :].rearrange("(t p) d -> p t d", p=P),
                            x[:, bass.ds(g * TG, TG), :]).then_inc(s_out, 16)
            e.wait_ge(s_out, 16 * GROUPS)

        @block.tensor
        def _(e):
            e.sem_inc(s_qkv, 1)
            e.wait_ge(s_const, 1)
            e.wait_ge(s_small, 16 * SMALL)

            def to_channels(src, g, dst=py):
                for t in range(TG):
                    ins = e.transpose(dst[:, t * P:(t + 1) * P], src[:, tile(g, t)], idf[:, :])
                ins.then_inc(s_xnT, 1)

            def gate_logits(l, g, src):
                for t in range(TG):
                    at = (g * TG + t) * NE
                    ins = e.matmul(po[:, at:at + NE], src[:, tile(g, t)] if l == 0 else
                                   src[:, t * P:(t + 1) * P], gate[:, l, :], start=True, stop=True)
                ins.then_inc(s_lg, 1)

            def ranks(l):
                e.wait_ge(s_mask, l + 1)
                e.matmul(pb[:, 0, 0:TILES * NE], upper[:, :], mask[:, :], start=True, stop=True)
                e.matmul(pb[:, 1, 0:TILES * NE], ones[:, :], mask[:, :], start=True, stop=True).then_inc(s_rank, 1)

            e.wait_ge(s_xn, 1)
            to_channels(work_all, 0)
            for g in range(GROUPS):
                e.wait_ge(s_xT, g + 1)
                if g > 0:
                    e.wait_ge(s_lowout, g)
                e.matmul(pb[0:RANK, 3, :], wdt[:, :], xT[:, group(g)], start=True, stop=True).then_inc(s_low, 1)
                if g > 0:
                    e.wait_ge(s_parts, g)
                e.matmul(pb[0:96, 2, :], wbc[:, :], xT[:, group(g)], start=True, stop=True).then_inc(s_bc, 1)
                gate_logits(0, g, xT)
                if g + 1 < GROUPS:
                    e.wait_ge(s_xn, g + 2)
                    to_channels(work_all, g + 1)
                e.wait_ge(s_lowout, g + 1)
                e.wait_ge(s_delta, g + 1)
                e.matmul(ph[:, :], wdp[:, :], low, start=True, stop=True).then_inc(s_pre, 1)
            ranks(0)
            e.wait_ge(s_slot, 1)

            def spread(g, n, bank, ready, c):
                e.matmul(pb[:, bank, :], pick[:, c + n:c + n + 1].to_broadcast([96, P]), parts[0:96, group(g)],
                         start=True, stop=True).then_inc(ready, 1)

            def b_row(g, n):
                if 2 <= n < 4:
                    e.wait_ge(s_bx, g * NS + (n - 1))
                spread(g, n, n % 2, s_bb, 0)

            def c_row(g, n):
                if n >= 2:
                    e.wait_ge(s_prod, g * NS + (n - 1))
                spread(g, n, 2 + n % 2, s_cb, NS)

            def y_sum(g, n):
                if n >= NS - 2:
                    e.wait_ge(s_prod, g * NS + (n + 1))
                if n == 0:
                    e.wait_ge(s_att, g + 1)
                e.matmul(py[:, :], idf[:, :], work[:, 4 + n % 2, :], start=(n == 0), stop=(n == NS - 1))\
                    .then_inc(s_ysum, 1)

            def block_turn(l, g, j):
                e.wait_ge(s_row[j % XR], turn(l, g, j) * 16 + 16)
                e.wait_ge(s_xrout, blockno(l, g, j) + 1)
                for k in range(2):
                    ins = e.transpose(px[:, k * D:(k + 1) * D], xrow[:, j % XR, k * D:(k + 1) * D], idh[:, :])
                ins.then_inc(s_xr, 1)

            block_expert = {}

            def block_up(l, g, j):
                en = block_expert[j] = expert(e, g, j)
                if j == BPG - 1:
                    e.wait_ge(s_xrout, blockno(l, g, j) + 2)
                e.wait_ge(s_gelu, blockno(l, g, j) + 1 - l)
                xh, xl = xrT[:, j % 2, 0:D], xrT[:, j % 2, D:2 * D]
                for c in range(HC):
                    at = bass.ds(en * HID + (l * NE * HID + c * P), P)
                    o = hidden(l, j)[:, c * P:(c + 1) * P]
                    e.matmul(o, w1h[:, at], xh, start=True, stop=False)
                    e.matmul(o, w1h[:, at], xl, start=False, stop=False)
                    ins = e.matmul(o, w1l[:, at], xh, start=False, stop=True)
                ins.then_inc(s_l1, 1)

            def block_down(l, g, j):
                en = block_expert[j]
                e.wait_ge(s_hl, blockno(l, g, j) + 3)
                e.wait_ge(s_res, blockno(l, g, j) + 1)
                for c in range(HC):
                    at = bass.ds(en * HID + (l * NE * HID + c * P), P)
                    hh, hl = hid_h[:, j % 2, c * P:(c + 1) * P], hid_l[:, j % 2, c * P:(c + 1) * P]
                    e.matmul(po[:, 0:D], hh, w2h[:, at], start=(c == 0), stop=False)
                    e.matmul(po[:, 0:D], hh, w2l[:, at], start=False, stop=False)
                    ins = e.matmul(po[:, 0:D], hl, w2h[:, at], start=False, stop=(c == HC - 1))
                ins.then_inc(s_l2, 1)

            def blocks_at(l, g, i):
                if i < BPG:
                    block_turn(l, g, i)
                if 1 <= i < 1 + BPG:
                    block_up(l, g, i - 1)
                if 3 <= i < 3 + BPG:
                    block_down(l, g, i - 3)

            def scan_group(g, with_blocks):
                b_row(g, 0)
                b_row(g, 1)
                for n in range(NS):
                    c_row(g, n)
                    if n + 2 < NS:
                        b_row(g, n + 2)
                    if n >= 2:
                        y_sum(g, n - 2)
                    if with_blocks:
                        blocks_at(0, g, n)
                y_sum(g, NS - 2)
                y_sum(g, NS - 1)
                e.wait_ge(s_yT, g + 1)
                for t in range(TG):
                    ins = e.transpose(py[:, t * P:(t + 1) * P], yT[:, t * P:(t + 1) * P], idf[:, :])
                ins.then_inc(s_yTT, 1)

            with e.Fori(0, FIRST) as g:
                scan_group(g, False)
            with e.Fori(FIRST, GROUPS) as g:
                scan_group(g, True)

            for g in range(GROUPS):
                e.wait_ge(s_xn, g + (GROUPS + 1))
                if g >= 2:
                    e.wait_ge(s_xT, g + (GROUPS - 1))
                to_channels(work_all, g, turned(g % 2))
            for g in range(GROUPS + 1):
                if g < GROUPS:
                    e.wait_ge(s_gb, g + 1)
                    e.wait_ge(s_xT, g + (2 * GROUPS - 1))
                    to_channels(big, g, turned(g % 2))
                if g > 0:
                    e.wait_ge(s_xT, g + 2 * GROUPS)
                    gate_logits(1, g - 1, xfT((g - 1) % 2))
            ranks(1)
            e.wait_ge(s_slot, 2)

            e.wait_ge(s_late, 48)

            def head_products(g):
                e.wait_ge(s_tran, g + 1)
                e.wait_ge(s_xg, g + 1)
                for t in range(TG):
                    ins = e.matmul(pb[:, t, 0:3 * D], xTg[:, t * P:(t + 1) * P], wqkv[:, :], start=True, stop=True)
                ins.then_inc(s_qkv, 1)

            def head_sum(g, quarter):
                if quarter == 0:
                    e.wait_ge(s_p1, g + 1)
                o = pb[:, 0, 0:TG * HD * HD].rearrange("p (t c) -> p t c", t=TG)
                for h in range(quarter * (HEADS // 4), (quarter + 1) * (HEADS // 4)):
                    ins = e.matmul(o, idf[:, :], product[:, 0, :, h * HD * HD:(h + 1) * HD * HD],
                                   start=(h == 0), stop=(h == HEADS - 1))
                if quarter == 3:
                    ins.then_inc(s_tsum, 1)

            def head_group(g, with_blocks, last=False):
                for i in range(STEPS):
                    if with_blocks:
                        blocks_at(1, g, i)
                    if 6 <= i < 10:
                        head_sum(g, i - 6)
                    if i == 12 and not last:
                        head_products(g + 1)

            head_products(0)
            with e.Fori(0, FIRST) as g:
                head_group(g, False)
            with e.Fori(FIRST, GROUPS - 1) as g:
                head_group(g, True)
            head_group(GROUPS - 1, True, last=True)

        @block.vector
        def _(e):
            st = Steps(e, s_dve)
            hold = hold_of(e, s_held[2])
            e.sem_inc(s_scan, NS)
            e.sem_inc(s_x1, BACK)
            e.sem_inc(s_hl, 2)
            for free in (s_delta, s_res, s_att, s_qks, s_tran):
                e.sem_inc(free, 1)

            def stats_of(src, g):
                for t in range(TG):
                    ins = e.bn_stats(stats[:, bass.ds(g * TG + t, 1), :].rearrange("p a c -> p (a c)"),
                                     src[:, tile(g, t)])
                return ins

            def moments(n):
                m_even, q_even, m_odd, q_odd = (stats[:, :, i] for i in (1, 2, 4, 5))
                e.tensor_tensor(mean[:, :], m_even, m_odd, ALU.add)
                st.seq(e.tensor_tensor(ntmp[:, :], m_even, m_odd, ALU.subtract))
                st.seq(e.tensor_tensor(ntmp[:, :], ntmp[:, :], ntmp[:, :], ALU.mult))
                st.seq(e.tensor_tensor(vare[:, :], q_even, q_odd, ALU.add))
                e.tensor_scalar(mean[:, :], mean[:, :], 0.5, None, ALU.mult)
                st.seq(e.tensor_scalar(vare[:, :], vare[:, :], 1.0 / D, LN_EPS, ALU.mult, ALU.add))
                e.scalar_tensor_tensor(out=vare[:, :], in0=ntmp[:, :], scalar=0.25, in1=vare[:, :],
                                       op0=ALU.mult, op1=ALU.add).then_inc(s_var, 1)
                e.wait_ge(s_rstd, n)
                st.seq(e.tensor_tensor(ntmp[:, :], rstd[:, :], rstd[:, :], ALU.mult))
                st.seq(e.tensor_tensor(ntmp[:, :], ntmp[:, :], vare[:, :], ALU.mult))
                st.seq(e.tensor_scalar(ntmp[:, :], ntmp[:, :], -0.5, 1.5, ALU.mult, ALU.add))
                st.seq(e.tensor_tensor(rstd[:, :], rstd[:, :], ntmp[:, :], ALU.mult))

            def normalise(dst, src, g):
                for t in range(TG):
                    ins = e.tensor_scalar(dst[:, tile(g, t)], src[:, tile(g, t)],
                                          mean[:, col(g * TG + t)],
                                          rstd[:, col(g * TG + t)], ALU.subtract, ALU.mult)
                return ins

            def route(l):
                full, scratch = [P, TILES, NE], [0]

                def place(n):
                    scratch[0] += n
                    return work_all[:, scratch[0] - n:scratch[0]]

                def tk(v):
                    return v.rearrange("p (t k) -> p t k", t=TILES)

                top, topi = tk(place(256)), tk(place(256).bitcast(U32))
                two, first, second, spare = tk(place(64)), tk(place(256)), tk(place(256)), tk(place(256))
                totals, upto, dest = tk(place(256)), tk(place(256)), tk(place(256))
                over, per, ends, base = (place(n) for n in (NE * TILES, NE, NE, NE))
                hits, hit = place(BLOCKS * NE), place(BLOCKS)
                slotf = place(2 * TILES).rearrange("p (k t) -> p k t", k=2)
                sums, second_e = place(TILES), place(TILES)
                for t in range(TILES):
                    ins = e.max(top[:, t, :], logits[:, t, :])
                st.seq(ins)
                for t in range(TILES):
                    ins = e.max_index(topi[:, t, :], top[:, t, :], logits[:, t, :])
                st.seq(ins)
                st.seq(e.tensor_copy(two, topi[:, :, 0:2]))
                number = count[:, 0:NE].unsqueeze(1).to_broadcast(full)
                e.tensor_tensor(first, number, two[:, :, 0:1].to_broadcast(full), ALU.is_equal)
                st.seq(e.tensor_tensor(second, number, two[:, :, 1:2].to_broadcast(full), ALU.is_equal))
                e.tensor_tensor(tk(mask[:, :]), first, second, ALU.add).then_inc(s_mask, 1)
                e.tensor_tensor(logits[:, :, :], logits[:, :, :], top[:, :, 0:1].to_broadcast(full),
                                ALU.subtract).then_inc(s_expin, 1)
                e.wait_ge(s_rank, l + 1)
                rank, tot = tk(pb[:, 0, 0:TILES * NE]), tk(pb[:, 1, 0:TILES * NE])
                st.seq(e.tensor_copy(totals, tot))
                for n in range(NE):
                    ins = e.tensor_tensor_scan(upto[:, :, n], ones[:, 0:TILES], totals[:, :, n], 0.0, ALU.mult, ALU.add)
                st.seq(ins)
                st.seq(e.tensor_scalar(base, upto[:, TILES - 1, :], 1.0 / P, None, ALU.mult))
                over3 = over.rearrange("p (k j) -> p k j", k=NE)
                st.seq(e.tensor_tensor(over3, base.unsqueeze(2).to_broadcast([P, NE, TILES]),
                                       count[:, 0:TILES].unsqueeze(1).to_broadcast([P, NE, TILES]), ALU.is_gt))
                st.seq(e.tensor_reduce(per, over3, AX_X, ALU.add))
                st.seq(e.tensor_tensor_scan(ends, ones[:, 0:NE], per, 0.0, ALU.mult, ALU.add))
                st.seq(e.tensor_tensor(base, ends, per, ALU.subtract))
                st.seq(e.tensor_scalar(base, base, float(P), None, ALU.mult))
                st.seq(e.tensor_tensor(dest, rank, upto, ALU.add))
                st.seq(e.tensor_tensor(dest, dest, totals, ALU.subtract))
                st.seq(e.tensor_tensor(dest, dest, base.unsqueeze(1).to_broadcast(full), ALU.add))
                for k, chosen in enumerate((first, second)):
                    st.seq(e.tensor_tensor(spare, chosen, dest, ALU.mult))
                    st.seq(e.tensor_reduce(slotf[:, k, :], spare, AX_X, ALU.add))
                st.seq(e.tensor_copy(slot[:, :, :], slotf))
                hits3 = hits[0:1, :].rearrange("p (b k) -> p b k", b=BLOCKS)
                st.seq(e.tensor_tensor(hits3, count[0:1, :].unsqueeze(2).to_broadcast([1, BLOCKS, NE]),
                                       ends[0:1, :].unsqueeze(1).to_broadcast([1, BLOCKS, NE]), ALU.is_ge))
                st.seq(e.tensor_reduce(hit[0:1, :], hits3, AX_X, ALU.add))
                e.tensor_scalar(eid[:, :], hit[0:1, :], float(NE - 1), None, ALU.min).then_inc(s_slot, 1)
                e.wait_ge(s_expout, l + 1)
                e.tensor_reduce(sums, logits[:, :, :], AX_X, ALU.add)
                st.seq(e.tensor_tensor(spare, second, logits[:, :, :], ALU.mult))
                st.seq(e.tensor_reduce(second_e, spare, AX_X, ALU.add))
                st.seq(e.scalar_tensor_tensor(out=sums, in0=sums, scalar=TOP_EPS[l], in1=second_e,
                                              op0=ALU.mult, op1=ALU.add))
                st.seq(e.tensor_scalar(sums, sums, 1.0, None, ALU.add))
                st.seq(e.reciprocal(topw[:, 0, :], sums))
                e.tensor_tensor(topw[:, 1, :], topw[:, 0, :], second_e, ALU.mult).then_inc(s_topw, 1)
                e.wait_ge(s_topw, l + 1)

            def combine(l, turn_, q):
                g = turn_ * BACK + q
                e.wait_ge(s_back[q], turn_ * 32 + (32 + l * (32 * GROUPS // BACK)))
                for k in range(2):
                    for t in range(TG):
                        at = x_all[:, tile(g, t)]
                        ins = e.scalar_tensor_tensor(out=at, in0=decay[:, 2 * q + k, t * D:(t + 1) * D],
                                                     scalar=topw[:, k, col(g * TG + t)], in1=at,
                                                     op0=ALU.mult, op1=ALU.add)
                    if k == 0:
                        st.seq(ins)
                ins.then_inc(s_x1, 1)
                e.wait_ge(s_x1, g + (BACK + 1 + l * GROUPS))

            e.wait_ge(s_x, 16)
            with st.loop(0, GROUPS, 1) as g:
                st.done(stats_of(x_all, g))
            st.wait()
            moments(1)
            e.wait_ge(s_const, 1)
            st.seq(e.tensor_copy(count[:, :], count_i[:, :]))
            e.wait_ge(s_aexp, 1)
            e.tensor_scalar(avec[:, :], avec[:, :], -1.0, None, ALU.mult).then_inc(s_avec, 1)

            def scan_input(g):
                e.wait_ge(s_bc, g + 1)
                hold()
                pg, left = parts[0:96, group(g)], hid[0:96, 0, :]
                st.seq(e.tensor_copy(pg, pb[0:96, 2, :]))
                e.tensor_tensor(left, pb[0:96, 2, :], pg, ALU.subtract).then_inc(s_parts, 1)
                e.wait_ge(s_parts, g + 1)
                hold()
                e.tensor_copy(parts[32:64, group(g)], hid[32:64, 0, :])
                st.seq(e.tensor_copy(parts[64:96, group(g)], hid[64:96, 0, :]))
                st.seq(e.tensor_tensor(hid[64:96, 0, :], hid[64:96, 0, :], parts[64:96, group(g)], ALU.subtract))
                hold()
                st.seq(e.tensor_copy(parts[64:96, group(g)], hid[64:96, 0, :]))
                e.wait_ge(s_soft, g + 1)
                st.seq(e.tensor_scalar(big[:, group(g)], ph[:, :], cols[:, 0:1], 0.0, ALU.add, ALU.max))
                e.tensor_tensor(big[:, group(g)], big[:, group(g)], tmp_b[:, :], ALU.add).then_inc(s_delta, 1)
                st.seq(e.engine_nop())

            AHEAD = 2
            for g in range(AHEAD):
                normalise(work_all, x_all, g).then_inc(s_xn, 1)
            with st.loop(0, GROUPS - AHEAD, 6) as g:
                normalise(work_all, x_all, g + AHEAD).then_inc(s_xn, 1)
                scan_input(g)
            for g in range(GROUPS - AHEAD, GROUPS):
                scan_input(g)
            e.wait_ge(s_rlo, GROUPS)
            e.wait_ge(s_lg, GROUPS)
            st.seq(e.tensor_copy(logits_all, po[:, 0:TILES * NE]))
            route(0)

            def block_split(l, g, j):
                e.wait_ge(s_gelu, blockno(l, g, j) + 2)
                st.seq(e.tensor_copy(hid_h[:, j % 2, :], hid[:, j % 2, :]))
                e.tensor_tensor(hid_l[:, j % 2, :], hid[:, j % 2, :], hid_h[:, j % 2, :], ALU.subtract).then_inc(s_hl, 1)

            def block_out(l, g, j):
                en = expert(e, g, j)
                e.wait_ge(s_l2, blockno(l, g, j) + 1)
                e.tensor_tensor(res[:, j % XR, :], po[:, 0:D], b2[:, bass.ds(en * D, D)], ALU.add).then_inc(s_res, 1)

            def blocks_at(l, g, i):
                if 4 <= i < 4 + BPG:
                    block_out(l, g, i - 4)
                if 2 <= i < 2 + BPG:
                    block_split(l, g, i - 2)

            def scan_group(g, with_blocks):
                dx = work[:, 6, :]
                st.seq(e.tensor_tensor(dx, big[:, group(g)], xT[:, group(g)], ALU.mult))

                def drive(n):
                    e.wait_ge(s_bb, g * NS + (n + 1))
                    if n >= 2:
                        e.wait_ge(s_scan, g * NS + (n - 1 + NS))
                    e.tensor_tensor(work[:, n % 2, :], dx, pb[:, n % 2, :], ALU.mult).then_inc(s_bx, 1)

                def scan(n):
                    e.wait_ge(s_a, g * NS + (n + 1))
                    e.wait_ge(s_bx, g * NS + (n + 1))
                    if n >= 2:
                        e.wait_ge(s_prod, g * NS + (n - 1))
                    for h in range(GC // SLEN):
                        sl = slice(h * SLEN, (h + 1) * SLEN)
                        ins = e.tensor_tensor_scan(work[:, 2 + n % 2, sl], decay[:, n, sl], work[:, n % 2, sl],
                                                   0.0, ALU.mult, ALU.add)
                    ins.then_inc(s_scan, 1)

                def weigh(n):
                    e.wait_ge(s_cb, g * NS + (n + 1))
                    e.wait_ge(s_scan, g * NS + (n + 1 + NS))
                    if n >= 2:
                        e.wait_ge(s_ysum, g * NS + (n - 1))
                    e.tensor_tensor(work[:, 4 + n % 2, :], work[:, 2 + n % 2, :], pb[:, 2 + n % 2, :],
                                    ALU.mult).then_inc(s_prod, 1)

                drive(0)
                for n in range(NS):
                    if n + 1 < NS:
                        drive(n + 1)
                    scan(n)
                    if n >= 1:
                        weigh(n - 1)
                    if with_blocks:
                        blocks_at(0, g, n)
                weigh(NS - 1)
                e.wait_ge(s_ysum, g * NS + NS)
                e.scalar_tensor_tensor(out=yT, in0=xT[:, group(g)], scalar=cols[:, 1:2], in1=py[:, :],
                                       op0=ALU.mult, op1=ALU.add).then_inc(s_yT, 1)
                e.wait_ge(s_yTT, g + 1)
                e.tensor_tensor(x_all[:, group(g)], x_all[:, group(g)], py[:, :], ALU.add).then_inc(s_att, 1)

            with st.loop(0, FIRST, 1) as g:
                scan_group(g, False)
            e.wait_ge(s_b2, 16)
            with st.loop(FIRST, GROUPS, 1 + BPG) as g:
                scan_group(g, True)

            with st.loop(0, GROUPS // BACK, 2 * BACK) as turn_:
                for q in range(BACK):
                    combine(0, turn_, q)
                    st.done(stats_of(x_all, turn_ * BACK + q))
            st.wait()
            moments(2)
            e.scalar_tensor_tensor(out=ntmp[:, :], in0=mean[:, :], scalar=-1.0, in1=rstd[:, :],
                                   op0=ALU.mult, op1=ALU.mult).then_inc(s_norm, 1)
            with st.loop(0, GROUPS, 1) as g:
                e.wait_ge(s_xn, g + (GROUPS + 1))
                hold()
                st.done(stats_of(work_all, g))
            st.wait()
            moments(3)
            e.wait_ge(s_late, 48)

            def experts_input(g, step):
                for t in range(TG):
                    at, i = tile(g, t), col(g * TG + t)
                    if step == 0:
                        ins = e.scalar_tensor_tensor(out=big[:, at], in0=work_all[:, at], scalar=mean[:, i],
                                                     in1=gb[:, 0, :], op0=ALU.subtract, op1=ALU.mult)
                    else:
                        ins = e.scalar_tensor_tensor(out=big[:, at], in0=big[:, at], scalar=rstd[:, i],
                                                     in1=gb[:, 1, :], op0=ALU.mult, op1=ALU.add)
                return ins

            experts_input(0, 0).then_inc(s_xf, 1)
            with e.Fori(0, GROUPS - 1) as g:
                experts_input(g + 1, 0).then_inc(s_xf, 1)
                e.wait_ge(s_xf, g + 1)
                hold()
                experts_input(g, 1).then_inc(s_gb, 1)
            e.wait_ge(s_xf, GROUPS)
            experts_input(GROUPS - 1, 1).then_inc(s_gb, 1)
            e.wait_ge(s_lg, 2 * GROUPS)
            st.seq(e.tensor_tensor(logits[:, :, :], po[:, 0:TILES * NE].rearrange("p (t k) -> p t k", t=TILES),
                                   bgate[:, :].unsqueeze(1).to_broadcast([P, TILES, NE]), ALU.add))
            e.wait_ge(s_add, GROUPS)
            route(1)

            q_, k_, v_, t_, o_ = (work[:, i, :] for i in range(5))
            qmax, kmax, qsum, ksum = (work[:, 5, i * 64:i * 64 + n] for i, n in enumerate((64, 32, 64, 32)))

            def heads_at(g, i):
                psq = pb[:, :, 0:D].rearrange("p t (h d) -> p t h d", d=HD)
                psk = pb[:, :, D:2 * D].rearrange("p t (h d) -> p t d h", d=HD)
                if i == 0:
                    e.wait_ge(s_v, g + 2)
                    e.tensor_reduce(qmax.rearrange("p (t h) -> p t h", t=TG), psq, AX_X, ALU.max)
                    st.seq(e.tensor_reduce(kmax.rearrange("p (t d) -> p t d", t=TG), psk, AX_X, ALU.max))
                    e.tensor_tensor(q_.rearrange("p (t h d) -> p t h d", t=TG, d=HD), psq,
                                    qmax.rearrange("p (t h) -> p t h", t=TG).unsqueeze(3).to_broadcast(
                                        [P, TG, HEADS, HD]), ALU.subtract).then_inc(s_qks, 1)
                    e.tensor_tensor(k_.rearrange("p (t h d) -> p t h d", t=TG, d=HD),
                                    pb[:, :, D:2 * D].rearrange("p t (h d) -> p t h d", d=HD),
                                    kmax.rearrange("p (t d) -> p t d", t=TG).unsqueeze(2).to_broadcast(
                                        [P, TG, HEADS, HD]), ALU.subtract).then_inc(s_qks, 1)
                if i == 2:
                    e.wait_ge(s_qke, g * 2 + 2)
                    e.tensor_reduce(qsum, q_.rearrange("p (c d) -> p c d", d=HD), AX_X, ALU.add)
                    st.seq(e.tensor_reduce(ksum.rearrange("p (t d) -> p t d", t=TG),
                                           k_.rearrange("p (t h d) -> p t d h", t=TG, d=HD), AX_X, ALU.add))
                    e.reciprocal(qsum, qsum)
                    st.seq(e.reciprocal(ksum, ksum))
                if 2 <= i < 2 + TG:
                    t = i - 2
                    full = [P, HEADS, HD, HD]
                    kt = k_[:, t * D:(t + 1) * D].rearrange("p (h d) -> p h d", d=HD).unsqueeze(3).to_broadcast(full)
                    vt = v_[:, t * D:(t + 1) * D].rearrange("p (h d) -> p h d", d=HD).unsqueeze(2).to_broadcast(full)
                    ins = e.tensor_tensor(product[:, 0, t, :].rearrange("p (h d c) -> p h d c", d=HD, c=HD),
                                          kt, vt, ALU.mult)
                    if t == TG - 1:
                        ins.then_inc(s_p1, 1)
                if i == 10:
                    e.wait_ge(s_tsum, g + 1)
                    e.tensor_tensor(t_[:, 0:TG * HD * HD].rearrange("p (c d) -> p c d", d=HD),
                                    pb[:, 0, 0:TG * HD * HD].rearrange("p (c d) -> p c d", d=HD),
                                    ksum.unsqueeze(2).to_broadcast([P, TG * HD, HD]), ALU.mult).then_inc(s_tran, 1)
                    e.wait_ge(s_tran, g + 2)
                if 10 <= i < 10 + TG:
                    t = i - 10
                    full = [P, HEADS, HD, HD]
                    qt = q_[:, t * D:(t + 1) * D].rearrange("p (h d) -> p h d", d=HD).unsqueeze(2).to_broadcast(full)
                    tt = t_[:, t * HD * HD:(t + 1) * HD * HD].rearrange("p (d c) -> p c d", d=HD)\
                        .unsqueeze(1).to_broadcast(full)
                    ins = e.tensor_tensor(product[:, 1, t, :].rearrange("p (h c d) -> p h c d", d=HD, c=HD),
                                          qt, tt, ALU.mult)
                    st.done(ins)
                if i == 10 + TG:
                    st.wait()
                    st.seq(e.tensor_reduce(o_, product[:, 1, :, :].rearrange("p t (c d) -> p (t c) d", d=HD),
                                           AX_X, ALU.add))
                    o3 = o_.rearrange("p (c d) -> p c d", d=HD)
                    st.seq(e.tensor_tensor(o3, o3, qsum.unsqueeze(2).to_broadcast([P, TG * HEADS, HD]), ALU.mult))
                    e.tensor_tensor(x_all[:, group(g)], x_all[:, group(g)], o_, ALU.add).then_inc(s_att, 1)

            with st.loop(0, FIRST, 9) as g:
                for i in range(STEPS):
                    heads_at(g, i)
            e.wait_ge(s_b2, 32)
            with st.loop(FIRST, GROUPS, 9 + BPG) as g:
                for i in range(STEPS):
                    heads_at(g, i)
                    blocks_at(1, g, i)
            with st.loop(0, GROUPS // BACK, BACK) as turn_:
                for q in range(BACK):
                    combine(1, turn_, q)


def kernel(**inputs):
    import numpy as np
    import concourse.bacc as bacc
    from concourse.bass_utils import run_bass_kernel_spmd

    L0, L1 = "L0_attn_", "L1_attn_"
    v = {k: np.asarray(w) for k, w in inputs.items()}

    def columns(b):
        return b.reshape(NE, HC, P).transpose(2, 0, 1).reshape(P, NE * HC)

    arrays = {
        "x": v[L0 + "x"].reshape(NTOK, D), "A_log": v[L0 + "A_log"], "D_param": v[L0 + "D_param"].reshape(D, 1),
        "W_bc": v[L0 + "W_bc"], "W_dt": v[L0 + "W_dt"], "W_dtproj": v[L0 + "W_dtproj"],
        "b_dt": v[L0 + "b_dtproj"].reshape(D, 1), "gate_0": v["L0_ffn_gate_w"].T, "gate_1": v["L1_ffn_Wg"].T,
        "w1_0": v["L0_ffn_w1"],
        "w2_0": v["L0_ffn_w2"].reshape(NE, HC, P, D).transpose(0, 2, 1, 3).reshape(NE, P, HID),
        "b1_0": columns(v["L0_ffn_b1"]), "b2_0": v["L0_ffn_b2"].reshape(1, NE * D),
        "wqkv": np.concatenate([v[L1 + "W_Q"].T, v[L1 + "W_K"].T, v[L1 + "W_V"].T], axis=1),
        "gamma": v["L1_ffn_gamma"].reshape(1, D), "beta": v["L1_ffn_beta"].reshape(1, D),
        "bg": v["L1_ffn_bg"].reshape(1, NE), "w1_1": v["L1_ffn_W1"].transpose(0, 2, 1),
        "w2_1": v["L1_ffn_W2"].reshape(NE, D, HC, P).transpose(0, 3, 2, 1).reshape(NE, P, HID),
        "b1_1": columns(v["L1_ffn_b1"]), "b2_1": v["L1_ffn_b2"].reshape(1, NE * D),
    }
    arrays = {k: np.ascontiguousarray(w) for k, w in arrays.items()}
    nc = bacc.Bacc("TRN2", target_bir_lowering=False, num_devices=1)
    aps = {k: nc.dram_tensor("in_" + k, w.shape, mybir.dt.from_np(w.dtype), kind="ExternalInput").ap()
           for k, w in arrays.items()}
    out = nc.dram_tensor("out", [NTOK, D], F32, kind="ExternalOutput").ap()
    build(nc, aps, out)
    r = run_bass_kernel_spmd(nc, [{"in_" + k: w for k, w in arrays.items()}], core_ids=[0])
    return r.results[0]["out"].reshape(SEQ, SLEN, D)
```

```python
from contextlib import ExitStack, contextmanager

import concourse.bass as bass
from concourse import mybir

ALU = mybir.AluOpType
ACT = mybir.ActivationFunctionType
AX_X = mybir.AxisListType.X
F32, F16, BF16 = mybir.dt.float32, mybir.dt.float16, mybir.dt.bfloat16
I32, U32 = mybir.dt.int32, mybir.dt.uint32

P = 128
SEQ, SLEN, D = 16, 256, 128
NTOK = SEQ * SLEN
TILES = NTOK // P
GROUPS = 8
TG = TILES // GROUPS
GC = TG * P
NS = 16
RANK = 64
NE = 8
HID = 512
HC = HID // P
HEADS, HD = 16, 8
LN_EPS = 1e-5
TOP_EPS = (1e-9, 1e-8)
BLOCKS = 72
FIRST = 2
BPG = BLOCKS // (GROUPS - FIRST)
ROWF = 2 * D + 2
DRAIN = 5
BACK = 4
HR = 3
DISP = 4
XIN = 4
XR = 6
assert BLOCKS >= 2 * TILES + NE - 1 and BPG % XR == 0 and BPG + DRAIN - 1 <= NS


class Steps:

    def __init__(self, eng, sem):
        self.eng, self.sem, self.n, self.off = eng, sem, 0, 0

    def done(self, ins):
        ins.then_inc(self.sem, 1)
        self.n += 1

    def wait(self):
        self.eng.wait_ge(self.sem, self.off + self.n)

    def seq(self, ins):
        self.done(ins)
        self.wait()

    @contextmanager
    def loop(self, first, end, per):
        n0 = self.n
        with self.eng.Fori(first, end) as i:
            self.off = (i - first) * per
            yield i
        assert self.n == n0 + per, (self.n - n0, per)
        self.n, self.off = n0 + per * (end - first), 0


def hold_of(eng, held):
    return lambda: eng.sem_inc(held, 1)


def build(nc, a, out):
    ctx = ExitStack()
    with ctx:
        def sb(name, shape, dt=F32):
            return ctx.enter_context(nc.sbuf_tensor(name, shape, dt))

        def ps(name, shape, dt=F32):
            return ctx.enter_context(nc.psum_tensor(name, shape, dt))

        def sem(name):
            return ctx.enter_context(nc.semaphore(name))

        def dram(name, shape, dt):
            return nc.dram_tensor(name, shape, dt, kind="Internal").ap()

        slots_dram = [dram(f"slots{l}", [BLOCKS * P, ROWF], F16) for l in range(2)]
        NRES = 2 * NTOK
        res_dram = [dram(f"results{l}", [NRES, D], F32) for l in range(2)]

        x = sb("x", [P, TILES, D])
        xT = sb("xT", [P, NTOK])
        big = sb("big", [P, NTOK])
        parts = sb("parts", [P, NTOK], BF16)
        rows = sb("rows", [P, TILES, ROWF], F16)
        decay = sb("decay", [P, NS, GC])
        work = sb("work", [P, 8, GC])
        w1h = sb("w1h", [P, 2 * NE * HID], F16)
        w1l = sb("w1l", [P, 2 * NE * HID], F16)
        w2 = sb("w2", [P, 2 * NE, HC, 2, D], F16)
        xrow = sb("xrow", [P, XR, ROWF], F16)
        xrT = sb("xrT", [P, 2, 2 * D], F16)
        hid = sb("hid", [P, 2, HID])
        hid_h = sb("hid_h", [P, HR, HID], F16)
        hid_l = sb("hid_l", [P, 2, HID], F16)
        res = sb("res", [P, XR, D])
        b1 = sb("b1", [P, 2 * NE * HC])
        idf = sb("idf", [P, P])
        idh = sb("idh", [P, P], F16)
        table = sb("table", [1, 1])
        ones_h = sb("ones_h", [1, P], F16)
        upper = sb("upper", [P, P], BF16)
        ones = sb("ones", [P, P], BF16)
        pick = sb("pick", [96, 2 * NS], BF16)
        wbc = sb("wbc", [P, 96])
        wdt = sb("wdt", [P, RANK])
        wdp = sb("wdp", [RANK, D])
        gate = sb("gate", [P, 2, NE])
        cols = sb("cols", [P, 2 + NS])
        avec = sb("avec", [P, NS])
        bgate = sb("bgate", [P, NE])
        stats = sb("stats", [P, TILES, 6])
        mean = sb("mean", [P, TILES])
        vare = sb("vare", [P, TILES])
        rstd = sb("rstd", [P, TILES])
        ntmp = sb("ntmp", [P, TILES])
        logits = sb("logits", [P, TILES, NE])
        mask = sb("mask", [P, TILES * NE], BF16)
        count_i = sb("count_i", [P, BLOCKS], I32)
        count = sb("count", [P, BLOCKS])
        topw = sb("topw", [P, 2, TILES])
        slot = sb("slot", [P, 2, TILES], I32)
        eid = sb("eid", [1, BLOCKS], I32)

        pb = ps("pb", [P, 4, GC])
        py = ps("py", [P, GC])
        px = ps("px", [P, 2 * D], F16)
        ph = ps("ph", [P, HID])
        po = ps("po", [P, GC])

        s_x = [sem(f"s_xin{i}") for i in range(XIN)]
        s_small = sem("s_small")
        s_late = sem("s_late")
        s_b2p = sem("s_b2p")
        s_b2 = sem("s_b2")
        s_stage = [sem(f"s_stage{i}") for i in range(8)]
        s_zeroed = [sem(f"s_zeroed{l}") for l in range(2)]
        s_disp = [[sem(f"s_disp{l}_{i}") for i in range(DISP)] for l in range(2)]
        s_row = [sem(f"s_row{i}") for i in range(XR)]
        s_sent = [sem(f"s_sent{i}") for i in range(XR)]
        s_back = [sem(f"s_back{i}") for i in range(BACK)]
        s_out = sem("s_out")
        s_pool = sem("s_pool")
        s_act = sem("s_act")
        s_dve = sem("s_dve")
        s_const = sem("s_const")
        s_held = [sem(f"s_held{i}") for i in range(3)]
        s_aexp = sem("s_aexp")
        s_avec = sem("s_avec")
        s_whi, s_wlo = sem("s_whi"), sem("s_wlo")
        s_var, s_rstd = sem("s_var"), sem("s_rstd")
        s_xn = sem("s_xn")
        s_xnT = sem("s_xnT")
        s_xT = sem("s_xT")
        s_lg = sem("s_lg")
        s_bc, s_parts = sem("s_bc"), sem("s_parts")
        s_low, s_lowout = sem("s_low"), sem("s_lowout")
        s_pre = sem("s_pre")
        s_abs, s_relu = sem("s_abs"), sem("s_relu")
        s_soft = sem("s_soft")
        s_delta = sem("s_delta")
        s_rhi = sem("s_rhi")
        s_rlo = sem("s_rlo")
        s_mask, s_rank = sem("s_mask"), sem("s_rank")
        s_expin, s_expout = sem("s_expin"), sem("s_expout")
        s_topw = sem("s_topw")
        s_slot = sem("s_slot")
        s_bb, s_cb = sem("s_bb"), sem("s_cb")
        s_bx = sem("s_bx")
        s_a = sem("s_a")
        s_scan = sem("s_scan")
        s_prod = sem("s_prod")
        s_ysum = sem("s_ysum")
        s_yT, s_yTT = sem("s_yT"), sem("s_yTT")
        s_att = sem("s_att")
        s_xr, s_xrout = sem("s_xr"), sem("s_xrout")
        s_l1, s_gelu, s_hl = sem("s_l1"), sem("s_gelu"), sem("s_hl")
        s_hh = sem("s_hh")
        s_l2, s_res = sem("s_l2"), sem("s_res")
        s_x1 = sem("s_x1")
        s_add = sem("s_add")
        s_norm = sem("s_norm")
        s_xf, s_gb = sem("s_xf"), sem("s_gb")
        s_xg = sem("s_xg")
        s_qkv, s_v = sem("s_qkv"), sem("s_v")
        s_qks, s_qke = sem("s_qks"), sem("s_qke")
        s_tran = sem("s_tran")
        s_p1, s_tsum = sem("s_p1"), sem("s_tsum")
        block = ctx.enter_context(nc.Block())

        decay_all = decay[:, :, :].rearrange("p a c -> p (a c)")
        stage = decay_all.rearrange("p (s c) -> p s c", s=8)
        rows_id = rows[:, :, :].rearrange("p t c -> p (t c)").bitcast(I32).rearrange(
            "p (t c) -> p t c", t=TILES)[:, :, D]
        w2_all = w2[:, :, :, :, :].rearrange("p n c k d -> p (n c k d)")
        rows_all = rows[:, :, :].rearrange("p t c -> p (t c)")
        b2 = rows_all.bitcast(F32)[0:1, 0:NE * D]
        b2_parts = rows_all[0:1, 2 * NE * D:4 * NE * D]
        parts_f = parts[:, :].bitcast(F32)
        wqkv = parts_f[:, 0:3 * D]
        gb = parts_f[:, 3 * D:5 * D].rearrange("p (k d) -> p k d", k=2)
        fill = xrow[:, 0, :]
        tmp_a = hid_h[:, 0:2, :].rearrange("p r c -> p (r c)").bitcast(F32)
        tmp_b = hid_l[:, :, :].rearrange("p r c -> p (r c)").bitcast(F32)
        yT = work[:, 7, :]
        xTg = work[:, 6, :]
        fill_id = fill[:, :].bitcast(I32)[:, D:D + 1]
        work_all = work[:, :, :].rearrange("p a c -> p (a c)")
        xn = work_all.rearrange("p (t c) -> p t c", c=D)
        x_all = x[:, :, :].rearrange("p t c -> p (t c)")
        xf = big[:, :].rearrange("p (t c) -> p t c", t=TILES)
        logits_all = logits[:, :, :].rearrange("p t k -> p (t k)")
        low = res[:, :, :].rearrange("p r c -> p (r c)")[0:RANK, 0:GC]
        product = decay_all.rearrange("p (k t c) -> p k t c", k=2, t=TG)
        SMALL = 13

        def ids_of(r):
            return xrow[:, r, :].bitcast(I32)[:, D:D + 1]

        def group(g):
            return bass.ds(g * GC, GC)

        def tile(g, t):
            return bass.ds(g * GC + t * P, P)

        def col(i):
            return bass.ds(i, 1)

        def blockno(l, g, j):
            return (g - FIRST) * BPG + (j + l * BLOCKS)

        def turn(l, g, j):
            return (g - FIRST) * (BPG // XR) + (j // XR + l * (BLOCKS // XR))

        def turned(par):
            return ph[:, :] if par else py[:, :]

        def xfT(par):
            return tmp_b[:, :] if par else tmp_a[:, :]

        def logs(g):
            return tmp_b[:, :] if g % 2 else tmp_a[:, :]

        def results(l, i):
            return big[:, i * GC:(i + 1) * GC] if l else decay[:, i, :]

        def block_of(i, lag, wrap):
            j = i - lag
            return j if (j >= 0 or wrap) and j < BPG else None

        def hidden(l, j):
            return py if l == 1 and j % 2 else ph

        def expert(e, g, j):
            return e.value_load(eid[0:1, col((g - FIRST) * BPG + j)], min_val=0, max_val=NE - 1)

        @block.sync
        def _(e):
            part = TILES // XIN
            for i in range(XIN):
                e.dma_start(x[:, i * part:(i + 1) * part, :],
                            a["x"][i * part * P:(i + 1) * part * P, :].rearrange("(t p) d -> p t d", p=P))\
                    .then_inc(s_x[i], 16)
            small = [(wbc[:, 32 * q:32 * q + 32], a["W_bc"]) for q in range(3)]
            small += [(wdt[:, :], a["W_dt"]), (wdp[:, :], a["W_dtproj"]), (gate[:, 0, :], a["gate_0"]),
                      (gate[:, 1, :], a["gate_1"]), (cols[:, 0:1], a["b_dt"]),
                      (cols[:, 1:2], a["D_param"]), (cols[:, 2:2 + NS], a["A_log"]),
                      (b1[:, 0:NE * HC], a["b1_0"]), (b1[:, NE * HC:2 * NE * HC], a["b1_1"]),
                      (bgate[:, :], a["bg"].to_broadcast([P, NE]))]
            assert len(small) == SMALL
            for dst, src in small:
                e.dma_start(dst, src).then_inc(s_small, 16)
            for i in range(2 * NE):
                l, n = i // NE, i % NE
                if i >= 8:
                    e.wait_ge(s_wlo, i - 7)
                e.dma_start(stage[:, i % 8, 0:HID], a[f"w1_{l}"][n]).then_inc(s_stage[i % 8], 16)
                e.dma_start(stage[:, i % 8, HID:2 * HID], a[f"w2_{l}"][n]).then_inc(s_stage[i % 8], 16)
            e.wait_ge(s_const, 1)
            for l in range(2):
                e.dma_start(slots_dram[l].rearrange("(b p) c -> p b c", p=P),
                            fill[:, :].unsqueeze(1).to_broadcast([P, BLOCKS, ROWF])).then_inc(s_zeroed[l], 16)

            for l in range(2):
                for i in range(DISP):
                    e.wait_ge(s_disp[l][i], 16 * 2 * TILES // DISP)
                e.dma_start(b2, a[f"b2_{l}"]).then_inc(s_b2, 16)

                def block_rows(g, j, used):
                    if used:
                        e.wait_ge(s_sent[j % XR], turn(l, g, j) * 16)
                    e.dma_start(xrow[:, j % XR, :], slots_dram[l][bass.ds(blockno(0, g, j) * P, P), :])\
                        .then_inc(s_row[j % XR], 16)

                for j in range(BPG):
                    block_rows(FIRST, j, l * BPG + j >= XR)
                with e.Fori(FIRST + 1, GROUPS) as g:
                    for j in range(BPG):
                        block_rows(g, j, True)
                for r in range(XR):
                    e.wait_ge(s_sent[r], 16 * (l + 1) * (BLOCKS // XR))
                if l == 0:
                    e.wait_ge(s_att, GROUPS + 1)
                    for dst, src in ((wqkv, a["wqkv"]), (gb[:, 0, :], a["gamma"].to_broadcast([P, D])),
                                     (gb[:, 1, :], a["beta"].to_broadcast([P, D]))):
                        e.dma_start(dst, src).then_inc(s_late, 16)
                with e.Fori(0, GROUPS // BACK) as turn_:
                    for q in range(BACK):
                        g = turn_ * BACK + q
                        e.wait_ge(s_x1, g + (1 + l * GROUPS))
                        for k in range(2):
                            e.dma_start(results(l, 2 * q + k).rearrange("p (t c) -> p t c", t=TG),
                                        res_dram[l][bass.ds(g * GC + k * NTOK, GC), :].rearrange(
                                            "(t p) c -> p t c", p=P)).then_inc(s_back[q], 16)

        @block.gpsimd
        def _(e):
            st = Steps(e, s_pool)
            hold = hold_of(e, s_held[0])
            e.memset(ones[:, :], 1.0)
            e.memset(ones_h[:, :], 1.0)
            e.memset(idf[:, :], 0.0)
            e.memset(idh[:, :], 0.0)
            e.memset(upper[:, :], 1.0)
            e.memset(pick[:, :], 0.0)
            e.iota(count_i[:, :], pattern=[[1, BLOCKS]], base=0, channel_multiplier=0)
            st.seq(e.memset(fill[:, :], 0.0))
            e.affine_select(out=idf[:, :], in_=idf[:, :], compare_op=ALU.not_equal, fill=1.0, base=0,
                            pattern=[[-1, P]], channel_multiplier=1)
            e.affine_select(out=idh[:, :], in_=idh[:, :], compare_op=ALU.not_equal, fill=1.0, base=0,
                            pattern=[[-1, P]], channel_multiplier=1)
            e.affine_select(out=upper[:, :], in_=upper[:, :], compare_op=ALU.is_gt, fill=0.0, base=0,
                            pattern=[[1, P]], channel_multiplier=-1)
            e.iota(fill_id, pattern=[[0, 1]], base=NRES, channel_multiplier=0)
            for q in range(3):
                st.seq(e.affine_select(out=pick[:, :], in_=pick[:, :], compare_op=ALU.not_equal, fill=1.0,
                                       base=-32 * q, pattern=[[-1, 2 * NS]], channel_multiplier=1))
            e.memset(eid[:, :], 0).then_inc(s_const, 1)
            def rows_low(l, g):
                hi, lo = (rows[:, bass.ds(g * TG, TG), k * D:(k + 1) * D] for k in range(2))
                e.tensor_tensor(lo, (xf if l else xn)[:, bass.ds(g * TG, TG), :], hi, ALU.subtract).then_inc(s_rlo, 1)

            for i in range(2 * NE):
                if i % 2 == 0:
                    e.wait_ge(s_rhi, i // 2 + 1)
                    rows_low(0, i // 2)
                e.wait_ge(s_whi, i + 1)
                sl = slice(i * HID, (i + 1) * HID)
                e.tensor_tensor(w1l[:, sl], stage[:, i % 8, 0:HID], w1h[:, sl], ALU.subtract)
                e.tensor_tensor(w2[:, i, :, 1, :], stage[:, i % 8, HID:2 * HID].rearrange("p (c d) -> p c d", c=HC),
                                w2[:, i, :, 0, :], ALU.subtract).then_inc(s_wlo, 1)

            for l in range(2):
                if l == 1:
                    with e.Fori(0, GROUPS) as g:
                        e.wait_ge(s_xn, g + (GROUPS + 1))
                        hold()
                        e.tensor_tensor(x_all[:, group(g)], x_all[:, group(g)], work_all[:, group(g)],
                                        ALU.add).then_inc(s_add, 1)
                    with e.Fori(0, GROUPS) as g:
                        e.wait_ge(s_rhi, g + (GROUPS + 1))
                        hold()
                        rows_low(1, g)
                st.seq(e.iota(rows_id, pattern=[[P, TILES]], base=0, channel_multiplier=1))
                e.wait_ge(s_rlo, (l + 1) * GROUPS)
                e.wait_ge(s_zeroed[l], 16)
                e.wait_ge(s_slot, l + 1)
                part = TILES // DISP
                for k in range(2):
                    for i in range(DISP):
                        if k == 1:
                            e.wait_ge(s_disp[l][i], 16 * part)
                            st.seq(e.iota(rows_id[:, i * part:(i + 1) * part], pattern=[[P, part]],
                                          base=NTOK + i * part * P, channel_multiplier=1))
                        for t in range(i * part, (i + 1) * part):
                            e.indirect_dma_start(slots_dram[l], bass.IndirectOffsetOnAxis(slot[:, k, t:t + 1], 0),
                                                 rows[:, t, :], None).then_inc(s_disp[l][i], 16)
                with e.Fori(FIRST, GROUPS) as g:
                    for j in range(BPG):
                        e.wait_ge(s_res, blockno(l, g, j) + 2)
                        hold()
                        e.indirect_dma_start(res_dram[l], bass.IndirectOffsetOnAxis(ids_of(j % XR), 0),
                                             res[:, j % XR, :], None, bounds_check=NRES - 1,
                                             oob_is_err=False).then_inc(s_sent[j % XR], 16)

        @block.scalar
        def _(e):
            st = Steps(e, s_act)
            hold = hold_of(e, s_held[1])
            for free in (s_xrout, s_gelu, s_v):
                e.sem_inc(free, 1)
            e.wait_ge(s_small, 16 * SMALL)
            e.activation(avec[:, :], cols[:, 2:2 + NS], ACT.Exp).then_inc(s_aexp, 1)

            def rstd_of(n):
                e.wait_ge(s_var, n)
                st.seq(e.activation(ntmp[:, :], vare[:, :], ACT.Ln))
                e.activation(rstd[:, :], ntmp[:, :], ACT.Exp, scale=-0.5).then_inc(s_rstd, 1)

            def gate_exp(n):
                e.wait_ge(s_expin, n)
                e.activation(logits_all, logits_all, ACT.Exp).then_inc(s_expout, 1)

            rstd_of(1)

            def channels_out(g):
                e.wait_ge(s_xnT, g + 1)
                e.copy(xT[:, group(g)], py[:, :]).then_inc(s_xT, 1)

            def rows_high(l, g):
                hi = rows[:, bass.ds(g * TG, TG), 0:D]
                if l == 0:
                    e.wait_ge(s_xn, g + 1)
                    e.copy(hi, xn[:, bass.ds(g * TG, TG), :]).then_inc(s_rhi, 1)
                else:
                    e.wait_ge(s_gb, g + 1)
                    hold()
                    e.copy(hi, xf[:, bass.ds(g * TG, TG), :]).then_inc(s_rhi, 1)

            def low_out(g):
                e.wait_ge(s_low, g + 1)
                if g > 0:
                    e.wait_ge(s_pre, g)
                e.copy(low, pb[0:RANK, 3, :]).then_inc(s_lowout, 1)

            def softplus(g):
                e.wait_ge(s_pre, g + 1)
                if g >= 2:
                    e.wait_ge(s_delta, g)
                e.activation(logs(g), ph[:, :], ACT.Abs, bias=cols[:, 0:1]).then_inc(s_abs, 1)
                if g % 2:
                    e.wait_ge(s_abs, g + 1)
                    for k in (g - 1, g):
                        st.done(e.activation(logs(k), logs(k), ACT.Exp, scale=-1.0))
                    st.wait()
                    for k in (g - 1, g):
                        e.activation(logs(k), logs(k), ACT.Ln, bias=1.0).then_inc(s_soft, 1)

            def weights_high(i):
                e.wait_ge(s_stage[i % 8], 32 * (i // 8 + 1))
                sl = slice(i * HID, (i + 1) * HID)
                e.copy(w1h[:, sl], stage[:, i % 8, 0:HID])
                e.copy(w2[:, i, :, 0, :], stage[:, i % 8, HID:2 * HID].rearrange("p (c d) -> p c d", c=HC))\
                    .then_inc(s_whi, 1)

            channels_out(0)
            for g in range(GROUPS):
                rows_high(0, g)
                low_out(g)
                weights_high(2 * g)
                if g + 1 < GROUPS:
                    channels_out(g + 1)
                softplus(g)
                weights_high(2 * g + 1)
            gate_exp(1)

            def table_for(function):
                st.seq(e.activation(table[:, :], avec[0:1, 0:1], function))

            def decay_of(g, n):
                e.wait_ge(s_scan, g * NS + (n + 1))
                hold()
                e.activation(decay[:, n, :], big[:, group(g)], ACT.Exp, scale=avec[:, n:n + 1]).then_inc(s_a, 1)

            def block_in(l, g, j):
                e.wait_ge(s_xr, blockno(l, g, j) + 1)
                e.copy(xrT[:, j % 2, :], px[:, :]).then_inc(s_xrout, 1)

            def block_gelu(l, g, j):
                en = expert(e, g, j)
                e.wait_ge(s_hl, blockno(l, g, j) + 1)
                e.wait_ge(s_l1, blockno(l, g, j) + 1)
                hold()
                for c in range(HC):
                    ins = e.activation(hid[:, j % 2, c * P:(c + 1) * P], hidden(l, j)[:, c * P:(c + 1) * P], ACT.Gelu,
                                       bias=b1[:, col(en * HC + (l * NE * HC + c))])
                ins.then_inc(s_gelu, 1)
                e.wait_ge(s_gelu, blockno(l, g, j) + 2)
                e.wait_ge(s_l2, blockno(l, g, j) + 1)
                e.copy(hid_h[:, j % HR, :], hid[:, j % 2, :]).then_inc(s_hh, 1)

            def blocks_at(l, g, i, wrap=False):
                for stage_of, lag in ((block_in, 0), (block_gelu, 1)):
                    j = block_of(i, lag, wrap)
                    if j is not None:
                        stage_of(l, g, j)

            def scan_group(g, with_blocks, last=False):
                if with_blocks:
                    for i in range(BPG + 1):
                        blocks_at(0, g, i)
                if not last:
                    for n in range(NS):
                        decay_of(g + 1, n)
                    table_for(ACT.Gelu)

            e.wait_ge(s_wlo, 2 * NE)
            e.wait_ge(s_avec, 1)
            for n in range(NS):
                decay_of(0, n)
            with st.loop(0, FIRST, 1) as g:
                scan_group(g, False)
            with st.loop(FIRST, GROUPS - 1, 1) as g:
                scan_group(g, True)
            scan_group(GROUPS - 1, True, last=True)

            rstd_of(2)

            def normalise(g):
                for t in range(TG):
                    ins = e.activation(work_all[:, tile(g, t)], x_all[:, tile(g, t)], ACT.Identity,
                                       bias=ntmp[:, col(g * TG + t)], scale=rstd[:, col(g * TG + t)])
                ins.then_inc(s_xn, 1)

            e.wait_ge(s_norm, 1)
            normalise(0)
            normalise(1)
            with e.Fori(0, GROUPS // 2 - 1) as pair:
                for par in range(2):
                    g = pair * 2 + par
                    e.wait_ge(s_xnT, g + (GROUPS + 1))
                    hold()
                    e.copy(xT[:, group(g)], turned(par)).then_inc(s_xT, 1)
                    normalise(g + 2)
            for g in range(GROUPS - 2, GROUPS):
                e.wait_ge(s_xnT, g + (GROUPS + 1))
                e.copy(xT[:, group(g)], turned(g % 2)).then_inc(s_xT, 1)
            rstd_of(3)
            with e.Fori(0, GROUPS // 2) as pair:
                for par in range(2):
                    g = pair * 2 + par
                    rows_high(1, g)
                    e.wait_ge(s_xnT, g + (2 * GROUPS + 1))
                    e.wait_ge(s_lg, g + (GROUPS - 1))
                    e.copy(xfT(par), turned(par)).then_inc(s_xT, 1)
            gate_exp(2)

            def head_input(g):
                e.wait_ge(s_qkv, g + 1)
                hold()
                e.copy(xTg, xT[:, group(g)]).then_inc(s_xg, 1)

            def v_out(g):
                e.wait_ge(s_qkv, g + 2)
                e.copy(work[:, 2, :].rearrange("p (t c) -> p t c", t=TG), pb[:, :, 2 * D:3 * D]).then_inc(s_v, 1)

            def head_exps(g):
                for k in range(2):
                    e.wait_ge(s_qks, g * 2 + (k + 2))
                    e.activation(work[:, k, :], work[:, k, :], ACT.Exp).then_inc(s_qke, 1)

            def head_group(g, with_blocks=True, wrap=True):
                for i in range(BPG):
                    if with_blocks:
                        blocks_at(1, g, i, wrap)
                    if i == 0:
                        head_input(g)
                    if i == 2:
                        v_out(g)
                    if i == 4:
                        head_exps(g)

            e.wait_ge(s_topw, 2)
            with e.Fori(0, FIRST) as g:
                head_group(g, with_blocks=False)
            head_group(FIRST, wrap=False)
            with e.Fori(FIRST + 1, GROUPS) as g:
                head_group(g)
            for i in range(BPG, BPG + DRAIN):
                blocks_at(1, GROUPS - 1, i)
            with e.Fori(0, GROUPS) as g:
                e.wait_ge(s_x1, g + (GROUPS + BACK + 1))
                e.dma_start(out[bass.ds(g * GC, GC), :].rearrange("(t p) d -> p t d", p=P),
                            x[:, bass.ds(g * TG, TG), :]).then_inc(s_out, 16)
            e.wait_ge(s_out, 16 * GROUPS)

        @block.tensor
        def _(e):
            e.sem_inc(s_qkv, 1)
            e.sem_inc(s_l2, HR)
            e.wait_ge(s_const, 1)
            e.wait_ge(s_small, 16 * SMALL)

            def to_channels(src, g, dst=py):
                for t in range(TG):
                    ins = e.transpose(dst[:, t * P:(t + 1) * P], src[:, tile(g, t)], idf[:, :])
                ins.then_inc(s_xnT, 1)

            def gate_logits(l, g, src):
                for t in range(TG):
                    at = (g * TG + t) * NE
                    ins = e.matmul(po[:, at:at + NE], src[:, tile(g, t)] if l == 0 else
                                   src[:, t * P:(t + 1) * P], gate[:, l, :], start=True, stop=True)
                ins.then_inc(s_lg, 1)

            def ranks(l):
                e.wait_ge(s_mask, l + 1)
                e.matmul(pb[:, 0, 0:TILES * NE], upper[:, :], mask[:, :], start=True, stop=True)
                e.matmul(pb[:, 1, 0:TILES * NE], ones[:, :], mask[:, :], start=True, stop=True).then_inc(s_rank, 1)

            e.wait_ge(s_xn, 1)
            to_channels(work_all, 0)
            for g in range(GROUPS):
                e.wait_ge(s_xT, g + 1)
                if g > 0:
                    e.wait_ge(s_lowout, g)
                e.matmul(pb[0:RANK, 3, :], wdt[:, :], xT[:, group(g)], start=True, stop=True).then_inc(s_low, 1)
                if g > 0:
                    e.wait_ge(s_parts, g)
                e.matmul(pb[0:96, 2, :], wbc[:, :], xT[:, group(g)], start=True, stop=True).then_inc(s_bc, 1)
                gate_logits(0, g, xT)
                if g + 1 < GROUPS:
                    e.wait_ge(s_xn, g + 2)
                    to_channels(work_all, g + 1)
                e.wait_ge(s_lowout, g + 1)
                if g > 0:
                    e.wait_ge(s_relu, g)
                e.matmul(ph[:, :], wdp[:, :], low, start=True, stop=True).then_inc(s_pre, 1)
            ranks(0)
            e.wait_ge(s_slot, 1)

            def spread(g, n, bank, ready, c):
                e.matmul(pb[:, bank, :], pick[:, c + n:c + n + 1].to_broadcast([96, P]), parts[0:96, group(g)],
                         start=True, stop=True).then_inc(ready, 1)

            def b_row(g, n):
                if 2 <= n < 4:
                    e.wait_ge(s_bx, g * NS + (n - 1))
                spread(g, n, n % 2, s_bb, 0)

            def c_row(g, n):
                if n >= 2:
                    e.wait_ge(s_prod, g * NS + (n - 1))
                spread(g, n, 2 + n % 2, s_cb, NS)

            def y_sum(g, n):
                if n >= NS - 2:
                    e.wait_ge(s_prod, g * NS + (n + 1))
                if n == 0:
                    e.wait_ge(s_att, g + 1)
                e.matmul(py[:, :], idf[:, :], work[:, 4 + n % 2, :], start=(n == 0), stop=(n == NS - 1))\
                    .then_inc(s_ysum, 1)

            def block_turn(l, g, j):
                e.wait_ge(s_row[j % XR], turn(l, g, j) * 16 + 16)
                e.wait_ge(s_xrout, blockno(l, g, j) + 1)
                for k in range(2):
                    ins = e.transpose(px[:, k * D:(k + 1) * D], xrow[:, j % XR, k * D:(k + 1) * D], idh[:, :])
                ins.then_inc(s_xr, 1)

            block_expert = {}

            def block_up(l, g, j):
                en = block_expert[j] = expert(e, g, j)
                if j == BPG - 1:
                    e.wait_ge(s_xrout, blockno(l, g, j) + 2)
                e.wait_ge(s_gelu, blockno(l, g, j) + 1 - l)
                xh, xl = xrT[:, j % 2, 0:D], xrT[:, j % 2, D:2 * D]
                for c in range(HC):
                    at = bass.ds(en * HID + (l * NE * HID + c * P), P)
                    o = hidden(l, j)[:, c * P:(c + 1) * P]
                    e.matmul(o, w1h[:, at], xh, start=True, stop=False)
                    e.matmul(o, w1h[:, at], xl, start=False, stop=False)
                    ins = e.matmul(o, w1l[:, at], xh, start=False, stop=True)
                ins.then_inc(s_l1, 1)

            def block_down(l, g, j):
                en = block_expert[j] if j >= 0 else expert(e, g, j)
                e.wait_ge(s_hl, blockno(l, g, j) + 3)
                e.wait_ge(s_res, blockno(l, g, j) + 1)
                both, high = po[:, 0:2 * D], po[:, 0:D]
                e.matmul(both, ones_h[:, :], b2_parts[:, bass.ds(en * (2 * D), 2 * D)], start=True, stop=False)
                for c in range(HC):
                    at = en * (2 * HID) + (l * NE * 2 * HID + c * 2 * D)
                    hh, hl = hid_h[:, j % HR, c * P:(c + 1) * P], hid_l[:, j % 2, c * P:(c + 1) * P]
                    e.matmul(high, hl, w2_all[:, bass.ds(at, D)], start=False, stop=False)
                    ins = e.matmul(both, hh, w2_all[:, bass.ds(at, 2 * D)], start=False, stop=(c == HC - 1))
                ins.then_inc(s_l2, 1)

            def blocks_at(l, g, i, wrap=False):
                for stage_of, lag in ((block_turn, 0), (block_up, 1), (block_down, 3)):
                    j = block_of(i, lag, wrap)
                    if j is not None:
                        stage_of(l, g, j)

            def to_tokens(g):
                e.wait_ge(s_yT, g + 1)
                for t in range(TG):
                    ins = e.transpose(py[:, t * P:(t + 1) * P], yT[:, t * P:(t + 1) * P], idf[:, :])
                ins.then_inc(s_yTT, 1)

            def scan_group(g, first=False, last=False, with_blocks=True):
                for n in range(NS):
                    c_row(g, n)
                    if n + 2 < NS:
                        b_row(g, n + 2)
                    elif not last:
                        b_row(g + 1, n + 2 - NS)
                    if with_blocks:
                        blocks_at(0, g, n)
                    if n >= 2:
                        y_sum(g, n - 2)
                    if n == 0 and not first:
                        to_tokens(g - 1)
                y_sum(g, NS - 2)
                y_sum(g, NS - 1)
                if last:
                    to_tokens(g)

            b_row(0, 0)
            b_row(0, 1)
            scan_group(0, first=True, with_blocks=False)
            for g in range(1, FIRST):
                scan_group(g, with_blocks=False)
            e.wait_ge(s_b2p, 1)
            with e.Fori(FIRST, GROUPS - 1) as g:
                scan_group(g)
            scan_group(GROUPS - 1, last=True)

            for g in range(GROUPS):
                e.wait_ge(s_xn, g + (GROUPS + 1))
                if g >= 2:
                    e.wait_ge(s_xT, g + (GROUPS - 1))
                to_channels(work_all, g, turned(g % 2))
            for g in range(GROUPS + 1):
                if g < GROUPS:
                    e.wait_ge(s_gb, g + 1)
                    e.wait_ge(s_xT, g + (2 * GROUPS - 1))
                    to_channels(big, g, turned(g % 2))
                if g > 0:
                    e.wait_ge(s_xT, g + 2 * GROUPS)
                    gate_logits(1, g - 1, xfT((g - 1) % 2))
            ranks(1)
            e.wait_ge(s_slot, 2)

            e.wait_ge(s_late, 48)

            def head_products(g):
                e.wait_ge(s_tran, g + 1)
                e.wait_ge(s_xg, g + 1)
                for t in range(TG):
                    ins = e.matmul(pb[:, t, 0:3 * D], xTg[:, t * P:(t + 1) * P], wqkv[:, :], start=True, stop=True)
                ins.then_inc(s_qkv, 1)

            def head_sum(g, quarter):
                if quarter == 0:
                    e.wait_ge(s_p1, g + 1)
                o = pb[:, 0, 0:TG * HD * HD].rearrange("p (t c) -> p t c", t=TG)
                for h in range(quarter * (HEADS // 4), (quarter + 1) * (HEADS // 4)):
                    ins = e.matmul(o, idf[:, :], product[:, 0, :, h * HD * HD:(h + 1) * HD * HD],
                                   start=(h == 0), stop=(h == HEADS - 1))
                if quarter == 3:
                    ins.then_inc(s_tsum, 1)

            def head_group(g, with_blocks=True, wrap=True):
                for i in range(BPG):
                    if with_blocks:
                        blocks_at(1, g, i, wrap)
                    if i == 1:
                        head_products(g)
                    if i >= BPG - 4:
                        head_sum(g, i - (BPG - 4))

            with e.Fori(0, FIRST) as g:
                head_group(g, with_blocks=False)
            e.wait_ge(s_b2p, 2)
            head_group(FIRST, wrap=False)
            with e.Fori(FIRST + 1, GROUPS) as g:
                head_group(g)
            for i in range(BPG, BPG + DRAIN):
                blocks_at(1, GROUPS - 1, i)

        @block.vector
        def _(e):
            st = Steps(e, s_dve)
            hold = hold_of(e, s_held[2])
            e.sem_inc(s_scan, NS)
            e.sem_inc(s_x1, BACK)
            e.sem_inc(s_hl, 2)
            for free in (s_delta, s_res, s_att, s_qks, s_tran):
                e.sem_inc(free, 1)

            def stats_of(src, g):
                for t in range(TG):
                    ins = e.bn_stats(stats[:, bass.ds(g * TG + t, 1), :].rearrange("p a c -> p (a c)"),
                                     src[:, tile(g, t)])
                return ins

            def moments(n):
                m_even, q_even, m_odd, q_odd = (stats[:, :, i] for i in (1, 2, 4, 5))
                e.tensor_tensor(mean[:, :], m_even, m_odd, ALU.add)
                st.seq(e.tensor_tensor(ntmp[:, :], m_even, m_odd, ALU.subtract))
                st.seq(e.tensor_tensor(ntmp[:, :], ntmp[:, :], ntmp[:, :], ALU.mult))
                st.seq(e.tensor_tensor(vare[:, :], q_even, q_odd, ALU.add))
                e.tensor_scalar(mean[:, :], mean[:, :], 0.5, None, ALU.mult)
                st.seq(e.tensor_scalar(vare[:, :], vare[:, :], 1.0 / D, LN_EPS, ALU.mult, ALU.add))
                e.scalar_tensor_tensor(out=vare[:, :], in0=ntmp[:, :], scalar=0.25, in1=vare[:, :],
                                       op0=ALU.mult, op1=ALU.add).then_inc(s_var, 1)
                e.wait_ge(s_rstd, n)
                st.seq(e.tensor_tensor(ntmp[:, :], rstd[:, :], rstd[:, :], ALU.mult))
                st.seq(e.tensor_tensor(ntmp[:, :], ntmp[:, :], vare[:, :], ALU.mult))
                st.seq(e.tensor_scalar(ntmp[:, :], ntmp[:, :], -0.5, 1.5, ALU.mult, ALU.add))
                st.seq(e.tensor_tensor(rstd[:, :], rstd[:, :], ntmp[:, :], ALU.mult))

            def normalise(dst, src, g):
                for t in range(TG):
                    ins = e.tensor_scalar(dst[:, tile(g, t)], src[:, tile(g, t)],
                                          mean[:, col(g * TG + t)],
                                          rstd[:, col(g * TG + t)], ALU.subtract, ALU.mult)
                return ins

            def route(l):
                full, scratch = [P, TILES, NE], [0]

                def place(n):
                    scratch[0] += n
                    return work_all[:, scratch[0] - n:scratch[0]]

                def tk(v):
                    return v.rearrange("p (t k) -> p t k", t=TILES)

                top, topi = tk(place(256)), tk(place(256).bitcast(U32))
                two, first, second, spare = tk(place(64)), tk(place(256)), tk(place(256)), tk(place(256))
                totals, upto, dest = tk(place(256)), tk(place(256)), tk(place(256))
                over, per, ends, base = (place(n) for n in (NE * TILES, NE, NE, NE))
                hits, hit = place(BLOCKS * NE), place(BLOCKS)
                slotf = place(2 * TILES).rearrange("p (k t) -> p k t", k=2)
                sums, second_e = place(TILES), place(TILES)
                for t in range(TILES):
                    ins = e.max(top[:, t, :], logits[:, t, :])
                st.seq(ins)
                for t in range(TILES):
                    ins = e.max_index(topi[:, t, :], top[:, t, :], logits[:, t, :])
                st.seq(ins)
                st.seq(e.tensor_copy(two, topi[:, :, 0:2]))
                number = count[:, 0:NE].unsqueeze(1).to_broadcast(full)
                e.tensor_tensor(first, number, two[:, :, 0:1].to_broadcast(full), ALU.is_equal)
                st.seq(e.tensor_tensor(second, number, two[:, :, 1:2].to_broadcast(full), ALU.is_equal))
                e.tensor_tensor(tk(mask[:, :]), first, second, ALU.add).then_inc(s_mask, 1)
                e.tensor_tensor(logits[:, :, :], logits[:, :, :], top[:, :, 0:1].to_broadcast(full),
                                ALU.subtract).then_inc(s_expin, 1)
                e.wait_ge(s_rank, l + 1)
                rank, tot = tk(pb[:, 0, 0:TILES * NE]), tk(pb[:, 1, 0:TILES * NE])
                st.seq(e.tensor_copy(totals, tot))
                for n in range(NE):
                    ins = e.tensor_tensor_scan(upto[:, :, n], ones[:, 0:TILES], totals[:, :, n], 0.0, ALU.mult, ALU.add)
                st.seq(ins)
                st.seq(e.tensor_scalar(base, upto[:, TILES - 1, :], 1.0 / P, None, ALU.mult))
                over3 = over.rearrange("p (k j) -> p k j", k=NE)
                st.seq(e.tensor_tensor(over3, base.unsqueeze(2).to_broadcast([P, NE, TILES]),
                                       count[:, 0:TILES].unsqueeze(1).to_broadcast([P, NE, TILES]), ALU.is_gt))
                st.seq(e.tensor_reduce(per, over3, AX_X, ALU.add))
                st.seq(e.tensor_tensor_scan(ends, ones[:, 0:NE], per, 0.0, ALU.mult, ALU.add))
                st.seq(e.tensor_tensor(base, ends, per, ALU.subtract))
                st.seq(e.tensor_scalar(base, base, float(P), None, ALU.mult))
                st.seq(e.tensor_tensor(dest, rank, upto, ALU.add))
                st.seq(e.tensor_tensor(dest, dest, totals, ALU.subtract))
                st.seq(e.tensor_tensor(dest, dest, base.unsqueeze(1).to_broadcast(full), ALU.add))
                for k, chosen in enumerate((first, second)):
                    st.seq(e.tensor_tensor(spare, chosen, dest, ALU.mult))
                    st.seq(e.tensor_reduce(slotf[:, k, :], spare, AX_X, ALU.add))
                st.seq(e.tensor_copy(slot[:, :, :], slotf))
                hits3 = hits[0:1, :].rearrange("p (b k) -> p b k", b=BLOCKS)
                st.seq(e.tensor_tensor(hits3, count[0:1, :].unsqueeze(2).to_broadcast([1, BLOCKS, NE]),
                                       ends[0:1, :].unsqueeze(1).to_broadcast([1, BLOCKS, NE]), ALU.is_ge))
                st.seq(e.tensor_reduce(hit[0:1, :], hits3, AX_X, ALU.add))
                e.tensor_scalar(eid[:, :], hit[0:1, :], float(NE - 1), None, ALU.min).then_inc(s_slot, 1)
                e.wait_ge(s_expout, l + 1)
                e.tensor_reduce(sums, logits[:, :, :], AX_X, ALU.add)
                st.seq(e.tensor_tensor(spare, second, logits[:, :, :], ALU.mult))
                st.seq(e.tensor_reduce(second_e, spare, AX_X, ALU.add))
                st.seq(e.scalar_tensor_tensor(out=sums, in0=sums, scalar=TOP_EPS[l], in1=second_e,
                                              op0=ALU.mult, op1=ALU.add))
                st.seq(e.tensor_scalar(sums, sums, 1.0, None, ALU.add))
                st.seq(e.reciprocal(topw[:, 0, :], sums))
                e.tensor_tensor(topw[:, 1, :], topw[:, 0, :], second_e, ALU.mult).then_inc(s_topw, 1)
                e.wait_ge(s_topw, l + 1)

            def combine(l, turn_, q):
                g = turn_ * BACK + q
                e.wait_ge(s_back[q], turn_ * 32 + (32 + l * (32 * GROUPS // BACK)))
                for k in range(2):
                    for t in range(TG):
                        at = x_all[:, tile(g, t)]
                        ins = e.scalar_tensor_tensor(out=at, in0=results(l, 2 * q + k)[:, t * D:(t + 1) * D],
                                                     scalar=topw[:, k, col(g * TG + t)], in1=at,
                                                     op0=ALU.mult, op1=ALU.add)
                    if k == 0:
                        st.seq(ins)
                ins.then_inc(s_x1, 1)
                e.wait_ge(s_x1, g + (BACK + 1 + l * GROUPS))

            for i in range(XIN):
                e.wait_ge(s_x[i], 16)
                for g in range(i * GROUPS // XIN, (i + 1) * GROUPS // XIN):
                    st.done(stats_of(x_all, g))
            st.wait()
            moments(1)
            e.wait_ge(s_const, 1)
            st.seq(e.tensor_copy(count[:, :], count_i[:, :]))
            e.wait_ge(s_aexp, 1)
            e.tensor_scalar(avec[:, :], avec[:, :], -1.0, None, ALU.mult).then_inc(s_avec, 1)

            def scan_input(g):
                e.wait_ge(s_bc, g + 1)
                hold()
                pg, left = parts[0:96, group(g)], hid[0:96, 0, :]
                st.seq(e.tensor_copy(pg, pb[0:96, 2, :]))
                e.tensor_tensor(left, pb[0:96, 2, :], pg, ALU.subtract).then_inc(s_parts, 1)
                e.wait_ge(s_parts, g + 1)
                hold()
                e.tensor_copy(parts[32:64, group(g)], hid[32:64, 0, :])
                st.seq(e.tensor_copy(parts[64:96, group(g)], hid[64:96, 0, :]))
                st.seq(e.tensor_tensor(hid[64:96, 0, :], hid[64:96, 0, :], parts[64:96, group(g)], ALU.subtract))
                hold()
                st.seq(e.tensor_copy(parts[64:96, group(g)], hid[64:96, 0, :]))

            def above_zero(g):
                e.wait_ge(s_abs, g + 1)
                hold()
                e.tensor_scalar(big[:, group(g)], ph[:, :], cols[:, 0:1], 0.0, ALU.add, ALU.max).then_inc(s_relu, 1)

            def soft(g, log):
                e.wait_ge(s_soft, g + 1)
                e.wait_ge(s_relu, g + 1)
                e.tensor_tensor(big[:, group(g)], big[:, group(g)], log, ALU.add).then_inc(s_delta, 1)
                st.seq(e.engine_nop())

            AHEAD = 2
            for g in range(AHEAD):
                normalise(work_all, x_all, g).then_inc(s_xn, 1)
            scan_input(0)
            above_zero(0)
            with st.loop(0, GROUPS // 2 - 1, 10) as pair:
                g = pair * 2
                normalise(work_all, x_all, g + 2).then_inc(s_xn, 1)
                scan_input(g + 1)
                above_zero(g + 1)
                normalise(work_all, x_all, g + 3).then_inc(s_xn, 1)
                scan_input(g + 2)
                for k in range(2):
                    soft(g + k, logs(k))
                above_zero(g + 2)
            scan_input(GROUPS - 1)
            above_zero(GROUPS - 1)
            for g in (GROUPS - 2, GROUPS - 1):
                soft(g, logs(g))
            e.wait_ge(s_rlo, GROUPS)
            e.wait_ge(s_lg, GROUPS)
            st.seq(e.tensor_copy(logits_all, po[:, 0:TILES * NE]))
            route(0)

            def block_split(l, g, j):
                e.wait_ge(s_hh, blockno(l, g, j) + 1)
                e.tensor_tensor(hid_l[:, j % 2, :], hid[:, j % 2, :], hid_h[:, j % HR, :], ALU.subtract)\
                    .then_inc(s_hl, 1)

            def block_out(l, g, j):
                e.wait_ge(s_l2, blockno(l, g, j) + (HR + 1))
                e.tensor_reduce(res[:, j % XR, :], po[:, 0:2 * D].rearrange("p (k d) -> p d k", k=2), AX_X, ALU.add)\
                    .then_inc(s_res, 1)

            def b2_in(l):
                e.wait_ge(s_b2, 16 * (l + 1))
                hi, lo = (b2_parts.rearrange("p (n k d) -> p n k d", n=NE, k=2)[:, :, k, :] for k in range(2))
                b = b2.rearrange("p (n d) -> p n d", n=NE)
                st.seq(e.tensor_copy(hi, b))
                e.tensor_tensor(lo, b, hi, ALU.subtract).then_inc(s_b2p, 1)

            def blocks_at(l, g, i, wrap=False):
                for stage_of, lag in ((block_out, 4), (block_split, 2)):
                    j = block_of(i, lag, wrap)
                    if j is not None:
                        stage_of(l, g, j)

            dx = work[:, 6, :]

            def drive(g, n):
                e.wait_ge(s_bb, g * NS + (n + 1))
                if n >= 2:
                    e.wait_ge(s_scan, g * NS + (n - 1 + NS))
                e.tensor_tensor(work[:, n % 2, :], dx, pb[:, n % 2, :], ALU.mult).then_inc(s_bx, 1)

            def scan(g, n):
                e.wait_ge(s_a, g * NS + (n + 1))
                e.wait_ge(s_bx, g * NS + (n + 1))
                if n >= 2:
                    e.wait_ge(s_prod, g * NS + (n - 1))
                for h in range(GC // SLEN):
                    sl = slice(h * SLEN, (h + 1) * SLEN)
                    ins = e.tensor_tensor_scan(work[:, 2 + n % 2, sl], decay[:, n, sl], work[:, n % 2, sl],
                                               0.0, ALU.mult, ALU.add)
                ins.then_inc(s_scan, 1)

            def weigh(g, n):
                e.wait_ge(s_cb, g * NS + (n + 1))
                e.wait_ge(s_scan, g * NS + (n + 1 + NS))
                if n >= 2:
                    e.wait_ge(s_ysum, g * NS + (n - 1))
                e.tensor_tensor(work[:, 4 + n % 2, :], work[:, 2 + n % 2, :], pb[:, 2 + n % 2, :],
                                ALU.mult).then_inc(s_prod, 1)

            def begin_scan(g):
                st.seq(e.tensor_tensor(dx, big[:, group(g)], xT[:, group(g)], ALU.mult))
                drive(g, 0)

            def end_scan(g):
                e.wait_ge(s_yTT, g + 1)
                e.tensor_tensor(x_all[:, group(g)], x_all[:, group(g)], py[:, :], ALU.add).then_inc(s_att, 1)

            def scan_group(g, first=False, last=False, with_blocks=True):
                for n in range(NS):
                    if n + 1 < NS:
                        drive(g, n + 1)
                    scan(g, n)
                    if with_blocks:
                        blocks_at(0, g, n)
                    if n >= 1:
                        weigh(g, n - 1)
                    if n == 1 and not first:
                        end_scan(g - 1)
                weigh(g, NS - 1)
                if not last:
                    begin_scan(g + 1)
                e.wait_ge(s_ysum, g * NS + NS)
                e.scalar_tensor_tensor(out=yT, in0=xT[:, group(g)], scalar=cols[:, 1:2], in1=py[:, :],
                                       op0=ALU.mult, op1=ALU.add).then_inc(s_yT, 1)
                if last:
                    end_scan(g)

            begin_scan(0)
            scan_group(0, first=True, with_blocks=False)
            for g in range(1, FIRST):
                scan_group(g, with_blocks=False)
            b2_in(0)
            with st.loop(FIRST, GROUPS - 1, 1) as g:
                scan_group(g)
            scan_group(GROUPS - 1, last=True)

            with st.loop(0, GROUPS // BACK, 2 * BACK) as turn_:
                for q in range(BACK):
                    combine(0, turn_, q)
                    st.done(stats_of(x_all, turn_ * BACK + q))
            st.wait()
            moments(2)
            e.scalar_tensor_tensor(out=ntmp[:, :], in0=mean[:, :], scalar=-1.0, in1=rstd[:, :],
                                   op0=ALU.mult, op1=ALU.mult).then_inc(s_norm, 1)
            with st.loop(0, GROUPS, 1) as g:
                e.wait_ge(s_xn, g + (GROUPS + 1))
                hold()
                st.done(stats_of(work_all, g))
            st.wait()
            moments(3)
            e.wait_ge(s_late, 48)

            def experts_input(g, step):
                for t in range(TG):
                    at, i = tile(g, t), col(g * TG + t)
                    if step == 0:
                        ins = e.scalar_tensor_tensor(out=big[:, at], in0=work_all[:, at], scalar=mean[:, i],
                                                     in1=gb[:, 0, :], op0=ALU.subtract, op1=ALU.mult)
                    else:
                        ins = e.scalar_tensor_tensor(out=big[:, at], in0=big[:, at], scalar=rstd[:, i],
                                                     in1=gb[:, 1, :], op0=ALU.mult, op1=ALU.add)
                return ins

            experts_input(0, 0).then_inc(s_xf, 1)
            with e.Fori(0, GROUPS - 1) as g:
                experts_input(g + 1, 0).then_inc(s_xf, 1)
                e.wait_ge(s_xf, g + 1)
                hold()
                experts_input(g, 1).then_inc(s_gb, 1)
            e.wait_ge(s_xf, GROUPS)
            experts_input(GROUPS - 1, 1).then_inc(s_gb, 1)
            e.wait_ge(s_lg, 2 * GROUPS)
            st.seq(e.tensor_tensor(logits[:, :, :], po[:, 0:TILES * NE].rearrange("p (t k) -> p t k", t=TILES),
                                   bgate[:, :].unsqueeze(1).to_broadcast([P, TILES, NE]), ALU.add))
            e.wait_ge(s_add, GROUPS)
            route(1)

            q_, k_, v_, t_, o_ = (work[:, i, :] for i in range(5))
            qmax, kmax, qsum, ksum = (work[:, 5, i * 64:i * 64 + n] for i, n in enumerate((64, 32, 64, 32)))

            full = [P, HEADS, HD, HD]

            def head_softmax(g, i):
                psq = pb[:, :, 0:D].rearrange("p t (h d) -> p t h d", d=HD)
                psk = pb[:, :, D:2 * D].rearrange("p t (h d) -> p t d h", d=HD)
                if i == 4:
                    e.wait_ge(s_v, g + 2)
                    e.tensor_reduce(qmax.rearrange("p (t h) -> p t h", t=TG), psq, AX_X, ALU.max)
                    st.seq(e.tensor_reduce(kmax.rearrange("p (t d) -> p t d", t=TG), psk, AX_X, ALU.max))
                    e.tensor_tensor(q_.rearrange("p (t h d) -> p t h d", t=TG, d=HD), psq,
                                    qmax.rearrange("p (t h) -> p t h", t=TG).unsqueeze(3).to_broadcast(
                                        [P, TG, HEADS, HD]), ALU.subtract).then_inc(s_qks, 1)
                    e.tensor_tensor(k_.rearrange("p (t h d) -> p t h d", t=TG, d=HD),
                                    pb[:, :, D:2 * D].rearrange("p t (h d) -> p t h d", d=HD),
                                    kmax.rearrange("p (t d) -> p t d", t=TG).unsqueeze(2).to_broadcast(
                                        [P, TG, HEADS, HD]), ALU.subtract).then_inc(s_qks, 1)
                if i == 5:
                    e.wait_ge(s_qke, g * 2 + 2)
                    e.tensor_reduce(qsum, q_.rearrange("p (c d) -> p c d", d=HD), AX_X, ALU.add)
                    st.seq(e.tensor_reduce(ksum.rearrange("p (t d) -> p t d", t=TG),
                                           k_.rearrange("p (t h d) -> p t d h", t=TG, d=HD), AX_X, ALU.add))
                    e.reciprocal(qsum, qsum)
                    st.seq(e.reciprocal(ksum, ksum))
                for t in {5: (0,), 6: (1,), 7: (2, 3)}.get(i, ()):
                    kt = k_[:, t * D:(t + 1) * D].rearrange("p (h d) -> p h d", d=HD).unsqueeze(3).to_broadcast(full)
                    vt = v_[:, t * D:(t + 1) * D].rearrange("p (h d) -> p h d", d=HD).unsqueeze(2).to_broadcast(full)
                    ins = e.tensor_tensor(product[:, 0, t, :].rearrange("p (h d c) -> p h d c", d=HD, c=HD),
                                          kt, vt, ALU.mult)
                    if t == TG - 1:
                        ins.then_inc(s_p1, 1)

            def head_out(g, i):
                if i == 0:
                    e.wait_ge(s_tsum, g + 1)
                    e.tensor_tensor(t_[:, 0:TG * HD * HD].rearrange("p (c d) -> p c d", d=HD),
                                    pb[:, 0, 0:TG * HD * HD].rearrange("p (c d) -> p c d", d=HD),
                                    ksum.unsqueeze(2).to_broadcast([P, TG * HD, HD]), ALU.mult).then_inc(s_tran, 1)
                    e.wait_ge(s_tran, g + 2)
                t = i - 1
                if 0 <= t < TG:
                    st.wait()
                    st.done(e.tensor_reduce(o_[:, t * D:(t + 1) * D],
                                            product[:, 1, t, :].rearrange("p (c d) -> p c d", d=HD), AX_X, ALU.add))
                t = i
                if 0 <= t < TG:
                    qt = q_[:, t * D:(t + 1) * D].rearrange("p (h d) -> p h d", d=HD).unsqueeze(2).to_broadcast(full)
                    tt = t_[:, t * HD * HD:(t + 1) * HD * HD].rearrange("p (d c) -> p c d", d=HD)\
                        .unsqueeze(1).to_broadcast(full)
                    st.done(e.tensor_tensor(product[:, 1, t, :].rearrange("p (h c d) -> p h c d", d=HD, c=HD),
                                            qt, tt, ALU.mult))
                if i == TG:
                    st.wait()
                    o3 = o_.rearrange("p (c d) -> p c d", d=HD)
                    st.seq(e.tensor_tensor(o3, o3, qsum.unsqueeze(2).to_broadcast([P, TG * HEADS, HD]), ALU.mult))
                    e.tensor_tensor(x_all[:, group(g)], x_all[:, group(g)], o_, ALU.add).then_inc(s_att, 1)

            def head_group(g, first=False, with_blocks=True, wrap=True):
                for i in range(BPG):
                    if with_blocks:
                        blocks_at(1, g, i, wrap)
                    if not first:
                        head_out(g - 1, i)
                    head_softmax(g, i)

            head_group(0, first=True, with_blocks=False)
            for g in range(1, FIRST):
                head_group(g, with_blocks=False)
            b2_in(1)
            head_group(FIRST, wrap=False)
            with st.loop(FIRST + 1, GROUPS, 12) as g:
                head_group(g)
            for i in range(DRAIN):
                blocks_at(1, GROUPS - 1, BPG + i)
                head_out(GROUPS - 1, i)
            with st.loop(0, GROUPS // BACK, BACK) as turn_:
                for q in range(BACK):
                    combine(1, turn_, q)


def kernel(**inputs):
    import numpy as np
    import concourse.bacc as bacc
    from concourse.bass_utils import run_bass_kernel_spmd

    L0, L1 = "L0_attn_", "L1_attn_"
    v = {k: np.asarray(w) for k, w in inputs.items()}

    def columns(b):
        return b.reshape(NE, HC, P).transpose(2, 0, 1).reshape(P, NE * HC)

    arrays = {
        "x": v[L0 + "x"].reshape(NTOK, D), "A_log": v[L0 + "A_log"], "D_param": v[L0 + "D_param"].reshape(D, 1),
        "W_bc": v[L0 + "W_bc"], "W_dt": v[L0 + "W_dt"], "W_dtproj": v[L0 + "W_dtproj"],
        "b_dt": v[L0 + "b_dtproj"].reshape(D, 1), "gate_0": v["L0_ffn_gate_w"].T, "gate_1": v["L1_ffn_Wg"].T,
        "w1_0": v["L0_ffn_w1"],
        "w2_0": v["L0_ffn_w2"].reshape(NE, HC, P, D).transpose(0, 2, 1, 3).reshape(NE, P, HID),
        "b1_0": columns(v["L0_ffn_b1"]), "b2_0": v["L0_ffn_b2"].reshape(1, NE * D),
        "wqkv": np.concatenate([v[L1 + "W_Q"].T, v[L1 + "W_K"].T, v[L1 + "W_V"].T], axis=1),
        "gamma": v["L1_ffn_gamma"].reshape(1, D), "beta": v["L1_ffn_beta"].reshape(1, D),
        "bg": v["L1_ffn_bg"].reshape(1, NE), "w1_1": v["L1_ffn_W1"].transpose(0, 2, 1),
        "w2_1": v["L1_ffn_W2"].reshape(NE, D, HC, P).transpose(0, 3, 2, 1).reshape(NE, P, HID),
        "b1_1": columns(v["L1_ffn_b1"]), "b2_1": v["L1_ffn_b2"].reshape(1, NE * D),
    }
    arrays = {k: np.ascontiguousarray(w) for k, w in arrays.items()}
    nc = bacc.Bacc("TRN2", target_bir_lowering=False, num_devices=1)
    aps = {k: nc.dram_tensor("in_" + k, w.shape, mybir.dt.from_np(w.dtype), kind="ExternalInput").ap()
           for k, w in arrays.items()}
    out = nc.dram_tensor("out", [NTOK, D], F32, kind="ExternalOutput").ap()
    build(nc, aps, out)
    r = run_bass_kernel_spmd(nc, [{"in_" + k: w for k, w in arrays.items()}], core_ids=[0])
    return r.results[0]["out"].reshape(SEQ, SLEN, D)
```
